# Optimizing a Trainium2 kernel written in Bass

```python
import numpy as np
import jax
import jax.numpy as jnp

def _softmax(x, axis=-1):
    return jax.nn.softmax(x, axis=axis)

def _gelu(x):
    return jax.nn.gelu(x, approximate=True)

def _silu(x):
    return jax.nn.silu(x)

def _sigmoid(x):
    return jax.nn.sigmoid(x)

def _layernorm(x, axis=-1, eps=1e-05):
    m = jnp.mean(x, axis=axis, keepdims=True)
    v = jnp.var(x, axis=axis, keepdims=True)
    return (x - m) / jnp.sqrt(v + eps)

def _scatter_add(tgt, idx, src, axis=0):
    return tgt.at[idx].add(src)

def _segment_sum(src, seg, n):
    return jax.ops.segment_sum(src, seg, n)
kernel_name = 'mk_gnn_resnorm_d2_gnn_r32_d57e47'

def setup_inputs(seed: int=0):
    np.random.seed(seed)
    _w = jnp.asarray

    def _rec_inputs():
        import jax
        import jax.numpy as jnp
        _gk = jax.random.key(seed)
        x = -0.0003713 + 1 * jax.random.normal(jax.random.fold_in(_gk, 1), (50000, 256), jnp.float32)
        src = jax.random.randint(jax.random.fold_in(_gk, 2), (50000,), 0, 50000, jnp.int32)
        dst = jnp.minimum((50000 * jax.random.uniform(jax.random.fold_in(_gk, 3), (50000,)) ** 2.0).astype(jnp.int32), 49999)
        _o = jnp.argsort(dst, stable=True)
        src = src[_o]
        dst = dst[_o]
        return (x, src, dst)
    x, src, dst = _rec_inputs()

    def _L0_gnn_setup():
        import jax, jax.numpy as jnp
        import numpy as np
        N_NODES = 50000
        N_EDGES = 10000
        DIM = 256
        key = jax.random.key(seed)
        ks = jax.random.split(key, 7)
        scale = 1.0 / np.sqrt(DIM)
        x = jax.random.normal(ks[0], (N_NODES, DIM), dtype=jnp.float32)
        edge_index = jax.random.randint(ks[1], (2, N_EDGES), 0, N_NODES, dtype=jnp.int64)
        W_key = jax.random.normal(ks[2], (DIM, DIM), dtype=jnp.float32) * scale
        W_query = jax.random.normal(ks[3], (DIM, DIM), dtype=jnp.float32) * scale
        W_value = jax.random.normal(ks[4], (DIM, DIM), dtype=jnp.float32) * scale
        W_skip = jax.random.normal(ks[5], (DIM, DIM), dtype=jnp.float32) * scale
        bias = jax.random.normal(ks[6], (DIM,), dtype=jnp.float32) * 0.01
        return {'x': x, 'edge_index': edge_index, 'W_key': W_key, 'W_query': W_query, 'W_value': W_value, 'W_skip': W_skip, 'bias': bias}
    _L0_gnn_all = _L0_gnn_setup()
    _L0_gnn_in = {k: v for k, v in _L0_gnn_all.items() if k in ('W_key', 'W_query', 'W_value', 'W_skip', 'bias')}
    del _L0_gnn_all

    def _L1_gnn_setup():
        import jax, jax.numpy as jnp
        import numpy as np
        N = 3125
        E = 50000
        D = 256
        BN_EPS = 1e-05
        key = jax.random.key(seed)
        ks = jax.random.split(key, 6)
        node_feats = jax.random.normal(ks[0], (N, D), dtype=jnp.float32)
        src = jax.random.randint(ks[1], (E,), 0, N, dtype=jnp.int64)
        dst = jax.random.randint(ks[2], (E,), 0, N, dtype=jnp.int64)
        eps = jnp.zeros((1,), dtype=jnp.float32)
        W1 = jax.random.normal(ks[3], (D, 2 * D), dtype=jnp.float32) * (1.0 / np.sqrt(D))
        b1 = jnp.zeros((2 * D,), dtype=jnp.float32)
        W2 = jax.random.normal(ks[4], (2 * D, D), dtype=jnp.float32) * (1.0 / np.sqrt(2 * D))
        b2 = jnp.zeros((D,), dtype=jnp.float32)
        gamma = jnp.ones((D,), dtype=jnp.float32)
        beta = jnp.zeros((D,), dtype=jnp.float32)
        return {'node_feats': node_feats, 'src': src, 'dst': dst, 'eps': eps, 'W1': W1, 'b1': b1, 'W2': W2, 'b2': b2, 'gamma': gamma, 'beta': beta}
    _L1_gnn_all = _L1_gnn_setup()
    _L1_gnn_in = {k: v for k, v in _L1_gnn_all.items() if k in ('eps', 'W1', 'b1', 'W2', 'b2', 'gamma', 'beta')}
    del _L1_gnn_all
    return {'x': x, 'src': src, 'dst': dst, 'L0_gnn_W_key': _L0_gnn_in['W_key'], 'L0_gnn_W_query': _L0_gnn_in['W_query'], 'L0_gnn_W_value': _L0_gnn_in['W_value'], 'L0_gnn_W_skip': _L0_gnn_in['W_skip'], 'L0_gnn_bias': _L0_gnn_in['bias'], 'L1_gnn_eps': _L1_gnn_in['eps'], 'L1_gnn_W1': _L1_gnn_in['W1'], 'L1_gnn_b1': _L1_gnn_in['b1'], 'L1_gnn_W2': _L1_gnn_in['W2'], 'L1_gnn_b2': _L1_gnn_in['b2'], 'L1_gnn_gamma': _L1_gnn_in['gamma'], 'L1_gnn_beta': _L1_gnn_in['beta']}

def reference(x, src, dst, L0_gnn_W_key, L0_gnn_W_query, L0_gnn_W_value, L0_gnn_W_skip, L0_gnn_bias, L1_gnn_eps, L1_gnn_W1, L1_gnn_b1, L1_gnn_W2, L1_gnn_b2, L1_gnn_gamma, L1_gnn_beta):
    import jax
    import jax.numpy as jnp

    def _L0_gnn_ref(x, edge_index, W_key, W_query, W_value, W_skip, bias):
        import jax, jax.numpy as jnp
        import numpy as np
        N_NODES = 50000
        N_EDGES = 10000
        DIM = 256
        src = edge_index[0]
        dst = edge_index[1]
        k = x @ W_key
        q = x @ W_query
        v = x @ W_value
        msg = jax.nn.sigmoid(k[dst] + q[src]) * v[src]
        agg = jax.ops.segment_sum(msg, dst, num_segments=x.shape[0])
        return agg + x @ W_skip + bias

    def _L1_gnn_ref(node_feats, src, dst, eps, W1, b1, W2, b2, gamma, beta):
        import jax, jax.numpy as jnp
        import numpy as np
        N = 3125
        E = 50000
        D = 256
        BN_EPS = 1e-05
        n = node_feats.shape[0]
        neigh = jax.ops.segment_sum(node_feats[src], dst, num_segments=n)
        h = (1.0 + eps) * node_feats + neigh
        h = jax.nn.relu(h @ W1 + b1) @ W2 + b2
        mean = jnp.mean(h, axis=0)
        var = jnp.mean(jnp.square(h - mean), axis=0)
        h = (h - mean) * jax.lax.rsqrt(var + BN_EPS) * gamma + beta
        return h
    edge_index = jnp.stack([src, dst])
    x = _layernorm(x + _L0_gnn_ref(x, edge_index, L0_gnn_W_key, L0_gnn_W_query, L0_gnn_W_value, L0_gnn_W_skip, L0_gnn_bias), axis=-1)
    x = _layernorm(x + _L1_gnn_ref(x, src, dst, L1_gnn_eps, L1_gnn_W1, L1_gnn_b1, L1_gnn_W2, L1_gnn_b2, L1_gnn_gamma, L1_gnn_beta), axis=-1)
    return x

_drawn_inputs = setup_inputs


def setup_inputs(seed=0):
    import zlib

    import numpy as np

    out = dict(_drawn_inputs(seed))
    spreads = {'L1_gnn_b1': (0.0, 0.1),
     'L1_gnn_b2': (0.0, 0.8),
     'L1_gnn_gamma': (1.0, 0.2),
     'L1_gnn_beta': (0.0, 0.1)}
    factors = {'L0_gnn_bias': 6.657}
    for name, (base, spread) in spreads.items():
        noise = np.random.default_rng([zlib.crc32(name.encode()), seed]).standard_normal(out[name].shape)
        drawn = base * np.exp(spread * noise) if base else spread * noise
        out[name] = jnp.asarray(drawn.astype(out[name].dtype))
    for name, factor in factors.items():
        out[name] = (out[name] * factor).astype(out[name].dtype)
    return out
```

```python
from contextlib import ExitStack

import concourse.bass as bass
from concourse import mybir

F32 = mybir.dt.float32
F32R = mybir.dt.float32r
I32 = mybir.dt.int32
ALU = mybir.AluOpType
ACT = mybir.ActivationFunctionType

P = 128
D = 256
KC = D // P
H = 512
HC = H // P
PR = 2 * P
SLOTS = 2
GATHERS = 4
HEAD = 8
EPS = 1e-5


def gnn_kernel(nc, x, gather_cols_in, dst_cols, dst_rows, w_key, w_query, w_value, w_skip,
               bias0, eps1, w1, b1, w2, b2, gamma, beta, out):
    N = x.shape[0]
    PAIRS = -(-N // PR)
    TAIL = N - (PAIRS - 1) * PR
    SPARE = N + 1
    ROWS = SPARE + PR
    assert TAIL <= P and dst_rows.shape[0] == PAIRS * PR

    base = nc.dram_tensor("base", (ROWS, D), F32, kind="Internal").ap()
    neigh = nc.dram_tensor("neigh", (ROWS, D), F32, kind="Internal").ap()
    x1_rows = nc.dram_tensor("x1_rows", (N, D), F32, kind="Internal").ap()
    h2_rows = nc.dram_tensor("h2_rows", (N, D), F32, kind="Internal").ap()

    def pair_steps(eng, lag=0, slots=SLOTS):
        loop_end = HEAD + (PAIRS - 1 - HEAD) // slots * slots
        for n in range(HEAD):
            yield n, n % slots
        with eng.Fori(HEAD, loop_end, slots) as i:
            for s in range(slots):
                yield i + s, s
        for n in range(loop_end, PAIRS + lag):
            yield n, n % slots

    def live(n):
        return not isinstance(n, int) or 0 <= n < PAIRS

    def late(n, k):
        return not isinstance(n, int) or n >= k

    def uses(n, s, dmas=1, slots=SLOTS):
        return (n - s) * (16 * dmas // slots) + 16 * dmas

    def used_before(n, s, dmas=1, slots=SLOTS):
        return (n - s) * (16 * dmas // slots)

    def last(n):
        return isinstance(n, int) and n == PAIRS - 1

    def node_rows(table, n):
        if last(n):
            return table[n * PR:n * PR + TAIL, :]
        return table[bass.ds(n * PR, PR), :].rearrange("(p r) d -> p r d", r=2)

    def node_tile(tile, n):
        return tile[0:TAIL, 0, :] if last(n) else tile[:, :, :]

    with ExitStack() as ctx:
        def sb(name, shape, dt=F32, c=ctx):
            return c.enter_context(nc.sbuf_tensor(name, shape, dt))

        def sems(c, *names):
            return [c.enter_context(nc.semaphore(name)) for name in names]

        def twice(row):
            return row[:, :].rearrange("p (a d) -> p a d", a=1).to_broadcast([P, 2, D])

        def ps(name, shape, c):
            return c.enter_context(nc.psum_tensor(name, shape, F32))

        def product(pe, target, terms, start=True, stop=True):
            for n, (a_hi, a_lo, b_hi, b_lo) in enumerate(terms):
                pe.matmul(target, a_hi, b_hi, start=(start and n == 0), stop=False)
                pe.matmul(target, a_hi, b_lo, start=False, stop=False)
                mm = pe.matmul(target, a_lo, b_hi, start=False, stop=(stop and n == len(terms) - 1))
            return mm

        def equal_edges(dve, m, q, dst_row, same, row_in, same_ok, summed_ok):
            dve.wait_ge(row_in, uses(m, q))
            if late(m, SLOTS):
                dve.wait_ge(summed_ok, m - 1)
            for j in range(2):
                eq = dve.tensor_scalar(same[:, j, :], dst_row[:, :], dst_f[:, bass.ds(2 * m + j, 1)], None, ALU.is_equal)
            eq.then_inc(same_ok, 1)

        def settle(eng):
            eng.sem_inc(settled, 1)

        def norm_buffers(c, stage):
            return ([sb(f"{stage}_stats{s}", [P, 2, 6], c=c) for s in range(SLOTS)],
                    [sb(f"{stage}_mean_var{s}", [P, 2, 2], c=c) for s in range(SLOTS)],
                    [sb(f"{stage}_root{s}", [P, 2], c=c) for s in range(SLOTS)],
                    [sb(f"{stage}_rstd{s}", [P, 2], c=c) for s in range(SLOTS)],
                    *sems(c, f"{stage}_stats_ok", f"{stage}_var_ok", f"{stage}_root_ok", f"{stage}_rstd_ok"))

        def norm_stats(dve, n, s, ln, rows):
            stats, mean_var, root, rstd, stats_ok, var_ok, root_ok, rstd_ok = ln
            for r in range(2):
                t = dve.bn_stats(stats[s][:, r, :], rows[:, r, :])
            t.then_inc(stats_ok, 1)
            dve.wait_ge(stats_ok, n + 1)
            settle(dve)
            for r in range(2):
                t = dve.bn_aggr(mean_var[s][:, r, :], stats[s][:, r, :])
            t.then_inc(var_ok, 1)

        def norm_root(act, n, s, ln):
            stats, mean_var, root, rstd, stats_ok, var_ok, root_ok, rstd_ok = ln
            act.wait_ge(var_ok, n + 1)
            act.activation(root[s][:, :], mean_var[s][:, :, 1], ACT.Sqrt, bias=eps_col[:, 0:1]).then_inc(root_ok, 1)

        def norm_apply(dve, n, s, ln, rows, target, target_ok):
            stats, mean_var, root, rstd, stats_ok, var_ok, root_ok, rstd_ok = ln
            dve.wait_ge(root_ok, n + 1)
            dve.reciprocal(rstd[s][:, :], root[s][:, :]).then_inc(rstd_ok, 1)
            dve.wait_ge(rstd_ok, n + 1)
            for r in range(2):
                t = dve.tensor_scalar(target[:, r, :], rows[:, r, :], mean_var[s][:, r, 0:1], rstd[s][:, r:r + 1],
                                      ALU.subtract, ALU.mult)
            t.then_inc(target_ok, 1)

        [settled] = sems(ctx, "settled")

        ident = sb("ident", [P, P])
        ones = sb("ones", [P, P])
        wqv = [sb(f"wqv_{q}", [P, KC, 2 * D], F32R) for q in ("hi", "lo")]
        wk = [sb(f"wk_{q}", [P, KC, D], F32R) for q in ("hi", "lo")]
        ws = [sb(f"ws_{q}", [P, KC, D], F32R) for q in ("hi", "lo")]
        w1s = [sb(f"w1_{q}", [P, KC, H], F32R) for q in ("hi", "lo")]
        w2s = [sb(f"w2_{q}", [P, HC, D], F32R) for q in ("hi", "lo")]
        bias0_b = sb("bias0_b", [P, D])
        b1_col = sb("b1_col", [P, HC])
        eps1_col = sb("eps1_col", [P, 1])
        eps_col = sb("eps_col", [P, 1])
        gather_cols = sb("gather_cols", [P, 4 * PAIRS], I32)
        dst_f = sb("dst_f", [P, 2 * PAIRS])
        scatter_i = sb("scatter_i", [P, 2 * PAIRS], I32)
        earlier = sb("earlier", [P, 2, PR])
        spare_f = sb("spare_f", [P, 2])
        zero = sb("zero", [P, 2, D])

        with ExitStack() as c:
            raw = sb("raw_w", [P, 4, 2 * D * KC], c=c)
            spare_i = sb("spare_i", [P, 2], I32, c)
            eps_raw = sb("eps_raw", [P, 1], c=c)
            dst_i = sb("dst_i", [P, 2 * PAIRS], I32, c)
            loaded, made, zero_made, split_hi, zeroed = sems(c, "loaded", "made", "zero_made", "split_hi", "zeroed")
            raw_v = raw[:, :, :]

            def raw_part(k, width, cols):
                return raw_v[:, k, :].rearrange("p (c n) -> p c n", n=width)[:, :, cols[0]:cols[1]]

            block = c.enter_context(nc.Block())

            @block.sync
            def _(sp):
                for k, width, cols, w in ((0, 2 * D, (0, D), w_query), (0, 2 * D, (D, 2 * D), w_value),
                                          (1, 2 * D, (0, D), w_key), (1, 2 * D, (D, 2 * D), w_skip),
                                          (2, H, (0, H), w1), (3, D, (0, D), w2)):
                    sp.dma_start(raw_part(k, width, cols), w.rearrange("(c p) n -> p c n", p=P)).then_inc(loaded, 16)
                for tile, array in ((bias0_b, bias0.rearrange("(a d) -> a d", a=1).to_broadcast([P, D])),
                                    (eps_raw, eps1.rearrange("(a d) -> a d", a=1).to_broadcast([P, 1])),
                                    (gather_cols, gather_cols_in), (dst_i, dst_cols)):
                    sp.dma_start(tile[:, :], array).then_inc(loaded, 16)
                with nc.allow_non_contiguous_dma(reason="512 biases, once"):
                    sp.dma_start(b1_col[:, :], b1.rearrange("(c p) -> p c", p=P)).then_inc(loaded, 16)
                sp.wait_ge(zero_made, 1)
                for first in range(N, ROWS, P):
                    count = min(P, ROWS - first)
                    sp.dma_start(base[first:first + count, :], zero[0:count, 0, :]).then_inc(zeroed, 16)
                sp.wait_ge(zeroed, 16 * -((N - ROWS) // P))

            @block.gpsimd
            def _(pool):
                pool.memset(ident[:, :], 0.0).then_inc(made, 1)
                pool.memset(ones[:, :], 1.0).then_inc(made, 1)
                pool.memset(earlier[:, :, :], 1.0).then_inc(made, 1)
                pool.wait_ge(made, 3)
                pool.affine_select(out=ident[:, :], in_=ident[:, :], compare_op=ALU.not_equal, fill=1.0, base=0,
                                   pattern=[[-1, P]], channel_multiplier=1).then_inc(made, 1)
                for t in range(2):
                    pool.affine_select(out=earlier[:, t, :], in_=earlier[:, t, :], compare_op=ALU.is_gt, fill=0.0,
                                       base=t * P, pattern=[[-1, PR]], channel_multiplier=1).then_inc(made, 1)
                pool.iota(spare_i[:, :], pattern=[[P, 2]], base=SPARE, channel_multiplier=1).then_inc(made, 1)

            @block.vector
            def _(dve):
                dve.memset(zero[:, :, :], 0.0).then_inc(zero_made, 1)
                dve.wait_ge(loaded, 16 * 11)
                parts = ((0, 2 * D, (0, 2 * D), wqv), (1, 2 * D, (0, D), wk), (1, 2 * D, (D, 2 * D), ws),
                         (2, H, (0, H), w1s), (3, D, (0, D), w2s))
                for k, width, cols, (hi, lo) in parts:
                    dve.tensor_copy(hi[:, :, :], raw_part(k, width, cols)).then_inc(split_hi, 1)
                for n, (k, width, cols, (hi, lo)) in enumerate(parts):
                    dve.wait_ge(split_hi, n + 1)
                    dve.tensor_tensor(lo[:, :, :], raw_part(k, width, cols), hi[:, :, :].bitcast(F32), ALU.subtract)
                dve.tensor_copy(dst_f[:, :], dst_i[:, :])
                dve.tensor_scalar(eps1_col[:, :], eps_raw[:, :], 1.0, None, ALU.add)
                dve.memset(eps_col[:, :], EPS)
                dve.wait_ge(made, 7)
                dve.tensor_copy(spare_f[:, :], spare_i[:, :])

        with ExitStack() as c:
            xt = [sb(f"a_x{s}", [P, 2, D], c=c) for s in range(GATHERS)]
            xb = [sb(f"a_xb{s}", [P, 2, D], c=c) for s in range(SLOTS)]
            res = [sb(f"a_res{s}", [P, 2, D], c=c) for s in range(SLOTS)]
            hi = [sb(f"a_hi{s}", [P, KC, PR], F32R, c) for s in range(SLOTS)]
            lo = [sb(f"a_lo{s}", [P, KC, PR], F32R, c) for s in range(SLOTS)]
            turned = [ps(f"a_turned{s}", [P, KC, PR], c) for s in range(SLOTS)]
            prod = [ps(f"a_prod{s}", [P, 2, D], c) for s in range(SLOTS)]
            x_in = sems(c, *(f"a_x_in{s}" for s in range(GATHERS)))
            stored = sems(c, *(f"a_stored{s}" for s in range(SLOTS)))
            turned_ok, hi_ok, lo_ok, prod_ok, xb_ok, res_ok = sems(
                c, "a_turned_ok", "a_hi_ok", "a_lo_ok", "a_prod_ok", "a_xb_ok", "a_res_ok")
            block = c.enter_context(nc.Block())

            @block.sync
            def _(sp):
                for n, g in pair_steps(sp, 5, GATHERS):
                    if live(n):
                        source = node_rows(x, n)
                        if late(n, GATHERS):
                            sp.wait_ge(turned_ok, n - 3)
                            sp.wait_ge(xb_ok, n - 3)
                        sp.dma_start(node_tile(xt[g], n), source).then_inc(x_in[g], 16)
                    m, q = n - 5, (g + 1) % SLOTS
                    if live(m):
                        target = node_rows(base, m)
                        sp.wait_ge(res_ok, m + 1)
                        sp.dma_start(target, node_tile(res[q], m)).then_inc(stored[q], 16)
                for s in range(SLOTS):
                    sp.wait_ge(stored[s], 16 * PAIRS // SLOTS)

            @block.tensor
            def _(pe):
                for n, g in pair_steps(pe, 1, GATHERS):
                    s = g % SLOTS
                    if live(n):
                        pe.wait_ge(x_in[g], uses(n, g, 1, GATHERS))
                        if late(n, SLOTS):
                            pe.wait_ge(lo_ok, n - 1)
                        for k in range(KC):
                            for r in range(2):
                                t = pe.transpose(turned[s][:, k, r * P:(r + 1) * P],
                                                 xt[g][:, r, k * P:(k + 1) * P], ident[:, :])
                        t.then_inc(turned_ok, 1)
                    m, q = n - 1, (s + 1) % SLOTS
                    if live(m):
                        pe.wait_ge(lo_ok, m + 1)
                        if late(m, SLOTS):
                            pe.wait_ge(res_ok, m - 1)
                        for r in range(2):
                            mm = product(pe, prod[q][:, r, :],
                                         [(hi[q][:, k, r * P:(r + 1) * P], lo[q][:, k, r * P:(r + 1) * P],
                                           ws[0][:, k, :], ws[1][:, k, :]) for k in range(KC)])
                        mm.then_inc(prod_ok, 1)

            @block.scalar
            def _(act):
                for n, s in pair_steps(act):
                    act.wait_ge(turned_ok, n + 1)
                    if late(n, SLOTS):
                        act.wait_ge(prod_ok, n - 1)
                    act.copy(hi[s][:, :, :], turned[s][:, :, :]).then_inc(hi_ok, 1)

            @block.gpsimd
            def _(pool):
                for n, g in pair_steps(pool, 0, GATHERS):
                    s = g % SLOTS
                    pool.wait_ge(x_in[g], uses(n, g, 1, GATHERS))
                    if late(n, SLOTS):
                        pool.wait_ge(res_ok, n - 1)
                    pool.tensor_tensor(xb[s][:, :, :], xt[g][:, :, :], twice(bias0_b), ALU.add).then_inc(xb_ok, 1)

            @block.vector
            def _(dve):
                for n, s in pair_steps(dve, 1):
                    if live(n):
                        dve.wait_ge(hi_ok, n + 1)
                        dve.tensor_tensor(lo[s][:, :, :], turned[s][:, :, :], hi[s][:, :, :].bitcast(F32),
                                          ALU.subtract).then_inc(lo_ok, 1)
                    m, q = n - 1, (s + 1) % SLOTS
                    if live(m):
                        dve.wait_ge(prod_ok, m + 1)
                        dve.wait_ge(xb_ok, m + 1)
                        if late(m, SLOTS):
                            dve.wait_ge(stored[q], used_before(m, q))
                        dve.tensor_tensor(res[q][:, :, :], prod[q][:, :, :], xb[q][:, :, :], ALU.add).then_inc(res_ok, 1)

        with ExitStack() as c:
            gather_i = [sb(f"b_gather_i{s}", [P, 2, 2], I32, c) for s in range(GATHERS)]
            xe = [sb(f"b_x{s}", [P, 2, 2, D], c=c) for s in range(GATHERS)]
            dst_row = [sb(f"b_dst_row{s}", [P, PR], I32, c) for s in range(SLOTS)]
            same = [sb(f"b_same{s}", [P, 2, PR], F32R, c) for s in range(SLOTS)]
            marked = sb("b_marked", [P, 2, PR], c=c)
            count = sb("b_count", [P, 2], c=c)
            to_spare = sb("b_to_spare", [P, 2], c=c)
            step = sb("b_step", [P, 2], c=c)
            scatter_slot = [sb(f"b_scatter_i{s}", [P, 2], I32, c) for s in range(GATHERS)]
            hi = [sb(f"b_hi{j}", [P, 2 * KC, P], F32R, c) for j in range(2)]
            lo = [sb(f"b_lo{j}", [P, 2 * KC, P], F32R, c) for j in range(2)]
            gate = [sb(f"b_gate{j}", [P, D], c=c) for j in range(2)]
            msg = [sb(f"b_msg{s}", [P, 2, D], c=c) for s in range(SLOTS)]
            msg_hi = [sb(f"b_msg_hi{s}", [P, 2, D], F32R, c) for s in range(SLOTS)]
            msg_lo = [sb(f"b_msg_lo{s}", [P, 2, D], F32R, c) for s in range(SLOTS)]
            rows = [sb(f"b_rows{s}", [P, 2, D], c=c) for s in range(GATHERS)]
            turned = [ps(f"b_turned{j}", [P, 2 * KC, P], c) for j in range(2)]
            prod = [[ps(f"b_prod{s}{j}", [P, 2 * D], c) for j in range(2)] for s in range(SLOTS)]
            summed = [ps(f"b_summed{s}", [P, 2, D], c) for s in range(SLOTS)]
            x_in = sems(c, *(f"b_x_in{s}" for s in range(GATHERS)))
            row_in = sems(c, *(f"b_row_in{s}" for s in range(SLOTS)))
            (zeroed, msg_hi_ok, msg_lo_ok, gather_i_ok, turned_ok, hi_ok, lo_ok, prod_ok, gate_ok, msg_ok, same_ok, marked_ok, index_ok,
             index_step, summed_ok, rows_ok, scattered) = sems(
                c, *("b_" + name for name in (
                    "zeroed msg_hi_ok msg_lo_ok gather_i_ok turned_ok hi_ok lo_ok prod_ok gate_ok msg_ok same_ok marked_ok index_ok "
                    "index_step summed_ok rows_ok scattered").split()))
            block = c.enter_context(nc.Block())

            @block.sync
            def _(sp):
                for n, s in pair_steps(sp):
                    source = dst_rows[bass.ds(n * PR, PR)].rearrange("(a e) -> a e", a=1).to_broadcast([P, PR])
                    if late(n, SLOTS):
                        sp.wait_ge(same_ok, n - 1)
                    sp.dma_start(dst_row[s][:, :], source).then_inc(row_in[s], 16)
                    first = PAIRS * PR if last(n) else n * PR
                    if last(n):
                        sp.dma_start(neigh[n * PR:(n + 1) * PR, :].rearrange("(p r) d -> p r d", r=2),
                                     zero[:, :, :]).then_inc(zeroed, 16)
                        sp.dma_start(neigh[first:ROWS, :], zero[0:ROWS - first, 0, :]).then_inc(zeroed, 16)
                    else:
                        sp.dma_start(neigh[bass.ds(first, PR), :].rearrange("(p r) d -> p r d", r=2),
                                     zero[:, :, :]).then_inc(zeroed, 16)
                sp.wait_ge(zeroed, 16 * (PAIRS + 1))

            @block.gpsimd
            def _(pool):
                for n, s in pair_steps(pool, 5, GATHERS):
                    if live(n):
                        pool.wait_ge(gather_i_ok, n + 1)
                        if late(n, GATHERS):
                            pool.wait_ge(turned_ok, 2 * n - 6)
                        settle(pool)
                        for e in range(2):
                            for j in range(2):
                                pool.indirect_dma_start(
                                    out=xe[s][:, e, j, :], out_offset=None, in_=x,
                                    in_offset=bass.IndirectOffsetOnAxis(ap=gather_i[s][:, e, j:j + 1], axis=0),
                                ).then_inc(x_in[s], 16)
                    m, q = n - 5, (s + 3) % GATHERS
                    if live(m):
                        pool.wait_ge(rows_ok, m + 1)
                        pool.wait_ge(index_ok, m + 1)
                        if late(m, 1):
                            pool.wait_ge(scattered, 32 * m)
                        settle(pool)
                        for j in range(2):
                            pool.indirect_dma_start(
                                out=base, out_offset=bass.IndirectOffsetOnAxis(ap=scatter_slot[q][:, j:j + 1], axis=0),
                                in_=rows[q][:, j, :], in_offset=None, compute_op=ALU.add).then_inc(scattered, 16)
                pool.wait_ge(scattered, 32 * PAIRS)

            @block.tensor
            def _(pe):
                for n, g in pair_steps(pe, 2, GATHERS):
                    if live(n):
                        pe.wait_ge(x_in[g], uses(n, g, 4, GATHERS))
                        for j in range(2):
                            if late(n, 1):
                                pe.wait_ge(lo_ok, 2 * n + j - 1)
                            for e in range(2):
                                for k in range(KC):
                                    t = pe.transpose(turned[j][:, e * KC + k, :],
                                                     xe[g][:, e, j, k * P:(k + 1) * P], ident[:, :])
                            t.then_inc(turned_ok, 1)
                    m, q = n - 1, (g + 1) % SLOTS
                    if live(m):
                        for j in range(2):
                            pe.wait_ge(lo_ok, 2 * m + j + 1)
                            if late(m, SLOTS):
                                pe.wait_ge(msg_ok, 2 * m + j - 3)
                            product(pe, prod[q][j][:, :],
                                    [(hi[j][:, k, :], lo[j][:, k, :], wqv[0][:, k, :], wqv[1][:, k, :])
                                     for k in range(KC)], stop=False)
                            mm = product(pe, prod[q][j][:, 0:D],
                                         [(hi[j][:, KC + k, :], lo[j][:, KC + k, :], wk[0][:, k, :], wk[1][:, k, :])
                                          for k in range(KC)], start=False)
                            mm.then_inc(prod_ok, 1)
                    m, q = n - 2, g % SLOTS
                    if live(m):
                        pe.wait_ge(msg_lo_ok, m + 1)
                        pe.wait_ge(same_ok, m + 1)
                        if late(m, SLOTS):
                            pe.wait_ge(rows_ok, m - 1)
                        for i in range(2):
                            for j in range(2):
                                pe.matmul(summed[q][:, i, :], same[q][:, j, i * P:(i + 1) * P], msg_hi[q][:, j, :],
                                          start=(j == 0), stop=False)
                                mm = pe.matmul(summed[q][:, i, :], same[q][:, j, i * P:(i + 1) * P], msg_lo[q][:, j, :],
                                               start=False, stop=(j == 1))
                        mm.then_inc(summed_ok, 1)

            @block.scalar
            def _(act):
                for n, s in pair_steps(act, 2, GATHERS):
                    m, q = n - 1, (s + 1) % SLOTS
                    for j in range(2):
                        if live(n):
                            act.wait_ge(turned_ok, 2 * n + j + 1)
                            if late(n, 1):
                                act.wait_ge(prod_ok, 2 * n + j - 1)
                            act.copy(hi[j][:, :, :], turned[j][:, :, :]).then_inc(hi_ok, 1)
                        if live(m):
                            act.wait_ge(prod_ok, 2 * m + j + 1)
                            if late(m, 1):
                                act.wait_ge(msg_ok, 2 * m + j - 1)
                            act.activation(gate[j][:, :], prod[q][j][:, 0:D], ACT.Sigmoid).then_inc(gate_ok, 1)
                    if live(m):
                        if late(m, SLOTS):
                            act.wait_ge(summed_ok, m - 1)
                        act.wait_ge(msg_ok, 2 * m + 2)
                        act.copy(msg_hi[q][:, :, :], msg[q][:, :, :]).then_inc(msg_hi_ok, 1)
                    m, q = n - 2, (s + 2) % GATHERS
                    if live(m):
                        act.wait_ge(summed_ok, m + 1)
                        if late(m, GATHERS):
                            act.wait_ge(scattered, 32 * (m - 3))
                        act.copy(rows[q][:, :, :], summed[q % SLOTS][:, :, :]).then_inc(rows_ok, 1)

            @block.vector
            def _(dve):
                for n, g in pair_steps(dve, 4, GATHERS):
                    if live(n):
                        if late(n, GATHERS):
                            dve.wait_ge(x_in[g], used_before(n, g, 4, GATHERS))
                        dve.tensor_copy(gather_i[g][:, :, :].rearrange("p e j -> p (e j)"),
                                        gather_cols[:, bass.ds(4 * n, 4)]).then_inc(gather_i_ok, 1)
                    ahead, m, q = n - 3, n - 4, g % SLOTS
                    for j in range(2):
                        if live(ahead):
                            dve.wait_ge(hi_ok, 2 * ahead + j + 1)
                            dve.tensor_tensor(lo[j][:, :, :], turned[j][:, :, :], hi[j][:, :, :].bitcast(F32),
                                              ALU.subtract).then_inc(lo_ok, 1)
                        if live(m):
                            dve.wait_ge(gate_ok, 2 * m + j + 1)
                            if late(m, SLOTS):
                                dve.wait_ge(msg_lo_ok, m - 1)
                            dve.tensor_tensor(msg[q][:, j, :], gate[j][:, :], prod[q][j][:, D:2 * D],
                                              ALU.mult).then_inc(msg_ok, 1)
                    if live(m):
                        equal_edges(dve, m, q, dst_row[q], same[q], row_in[q], same_ok, summed_ok)
                        dve.wait_ge(same_ok, m + 1)
                        if late(m, 1):
                            dve.wait_ge(index_ok, m)
                        for j in range(2):
                            mark = dve.tensor_tensor_reduce(marked[:, j, :], same[q][:, j, :].bitcast(F32), earlier[:, j, :], 1.0, 0.0,
                                                            ALU.mult, ALU.add, count[:, j:j + 1])
                        mark.then_inc(index_step, 1)
                        dve.tensor_tensor(to_spare[:, :], spare_f[:, :], dst_f[:, bass.ds(2 * m, 2)],
                                          ALU.subtract).then_inc(index_step, 1)
                        dve.wait_ge(index_step, 3 * m + 2)
                        dve.scalar_tensor_tensor(step[:, :], count[:, :], 0.0, to_spare[:, :], ALU.is_gt,
                                                 ALU.mult).then_inc(index_step, 1)
                        dve.wait_ge(index_step, 3 * m + 3)
                        if late(m, GATHERS):
                            dve.wait_ge(scattered, 32 * (m - 3))
                        dve.tensor_tensor(scatter_i[:, bass.ds(2 * m, 2)], step[:, :], dst_f[:, bass.ds(2 * m, 2)], ALU.add)
                        dve.tensor_tensor(scatter_slot[g][:, :], step[:, :], dst_f[:, bass.ds(2 * m, 2)],
                                          ALU.add).then_inc(index_ok, 1)
                        dve.wait_ge(msg_hi_ok, m + 1)
                        dve.tensor_tensor(msg_lo[q][:, :, :], msg[q][:, :, :], msg_hi[q][:, :, :].bitcast(F32),
                                          ALU.subtract).then_inc(msg_lo_ok, 1)

        with ExitStack() as c:
            gather_i = [sb(f"c_gather_i{s}", [P, 2], I32, c) for s in range(GATHERS)]
            scatter_slot = [sb(f"c_scatter_i{s}", [P, 2], I32, c) for s in range(GATHERS)]
            xe = [sb(f"c_x{s}", [P, 2, D], c=c) for s in range(GATHERS)]
            dst_row = [sb(f"c_dst_row{s}", [P, PR], I32, c) for s in range(SLOTS)]
            same = [sb(f"c_same{s}", [P, 2, PR], c=c) for s in range(SLOTS)]
            normed = [sb(f"c_normed{s}", [P, 2, D], c=c) for s in range(SLOTS)]
            rows = [sb(f"c_rows{s}", [P, 2, D], c=c) for s in range(GATHERS)]
            summed = [ps(f"c_summed{s}", [P, 2, D], c) for s in range(SLOTS)]
            ln = norm_buffers(c, "c")
            x_in = sems(c, *(f"c_x_in{s}" for s in range(GATHERS)))
            row_in = sems(c, *(f"c_row_in{s}" for s in range(SLOTS)))
            (gather_i_ok, same_ok, index_ok, normed_ok, summed_ok, rows_ok, scattered) = sems(
                c, *("c_" + name for name in (
                    "gather_i_ok same_ok index_ok normed_ok summed_ok rows_ok scattered").split()))
            block = c.enter_context(nc.Block())

            @block.sync
            def _(sp):
                for n, s in pair_steps(sp):
                    source = dst_rows[bass.ds(n * PR, PR)].rearrange("(a e) -> a e", a=1).to_broadcast([P, PR])
                    if late(n, SLOTS):
                        sp.wait_ge(same_ok, n - 1)
                    sp.dma_start(dst_row[s][:, :], source).then_inc(row_in[s], 16)

            @block.gpsimd
            def _(pool):
                for n, s in pair_steps(pool, 5, GATHERS):
                    if live(n):
                        pool.wait_ge(gather_i_ok, n + 1)
                        if late(n, GATHERS):
                            pool.wait_ge(normed_ok, n - 3)
                        settle(pool)
                        for j in range(2):
                            pool.indirect_dma_start(
                                out=xe[s][:, j, :], out_offset=None, in_=base,
                                in_offset=bass.IndirectOffsetOnAxis(ap=gather_i[s][:, j:j + 1], axis=0),
                            ).then_inc(x_in[s], 16)
                    m, q = n - 5, (s + 3) % GATHERS
                    if live(m):
                        pool.wait_ge(rows_ok, m + 1)
                        pool.wait_ge(index_ok, m + 1)
                        if late(m, 1):
                            pool.wait_ge(scattered, 32 * m)
                        settle(pool)
                        for j in range(2):
                            pool.indirect_dma_start(
                                out=neigh, out_offset=bass.IndirectOffsetOnAxis(ap=scatter_slot[q][:, j:j + 1], axis=0),
                                in_=rows[q][:, j, :], in_offset=None, compute_op=ALU.add).then_inc(scattered, 16)
                pool.wait_ge(scattered, 32 * PAIRS)

            @block.tensor
            def _(pe):
                for n, s in pair_steps(pe):
                    pe.wait_ge(normed_ok, n + 1)
                    pe.wait_ge(same_ok, n + 1)
                    if late(n, SLOTS):
                        pe.wait_ge(rows_ok, n - 1)
                    for i in range(2):
                        for j in range(2):
                            mm = pe.matmul(summed[s][:, i, :], same[s][:, j, i * P:(i + 1) * P], normed[s][:, j, :],
                                           start=(j == 0), stop=(j == 1))
                    mm.then_inc(summed_ok, 1)

            @block.scalar
            def _(act):
                for n, g in pair_steps(act, 1, GATHERS):
                    s = g % SLOTS
                    if live(n):
                        norm_root(act, n, s, ln)
                    m, q = n - 1, (g + 3) % GATHERS
                    if live(m):
                        act.wait_ge(summed_ok, m + 1)
                        if late(m, GATHERS):
                            act.wait_ge(scattered, 32 * (m - 3))
                        act.copy(rows[q][:, :, :], summed[q % SLOTS][:, :, :]).then_inc(rows_ok, 1)

            @block.vector
            def _(dve):
                for n, s in pair_steps(dve, 3, GATHERS):
                    if live(n):
                        if late(n, GATHERS):
                            dve.wait_ge(x_in[s], used_before(n, s, 2, GATHERS))
                        dve.tensor_copy(gather_i[s][:, :], gather_cols[:, bass.ds(4 * n, 2)]).then_inc(gather_i_ok, 1)
                    m, g, q = n - 3, (s + 1) % GATHERS, (s + 1) % SLOTS
                    if live(m):
                        dve.wait_ge(x_in[g], uses(m, g, 2, GATHERS))
                        norm_stats(dve, m, q, ln, xe[g])
                        if late(m, GATHERS):
                            dve.wait_ge(scattered, 32 * (m - 3))
                        dve.tensor_copy(scatter_slot[g][:, :], scatter_i[:, bass.ds(2 * m, 2)]).then_inc(index_ok, 1)
                        equal_edges(dve, m, q, dst_row[q], same[q], row_in[q], same_ok, summed_ok)
                        norm_apply(dve, m, q, ln, xe[g], normed[q], normed_ok)

        h2_sum = sb("h2_sum", [P, 2, D])
        h2_squares = sb("h2_squares", [P, 2, D])
        with ExitStack() as c:
            bt = [sb(f"d_base{s}", [P, 2, D], c=c) for s in range(SLOTS)]
            nt = [sb(f"d_neigh{s}", [P, 2, D], c=c) for s in range(SLOTS)]
            x1 = [sb(f"d_x1{s}", [P, 2, D], c=c) for s in range(SLOTS)]
            h = [sb(f"d_h{s}", [P, 2, D], c=c) for s in range(SLOTS)]
            hi = [sb(f"d_hi{s}", [P, KC, PR], F32R, c) for s in range(SLOTS)]
            lo = [sb(f"d_lo{s}", [P, KC, PR], F32R, c) for s in range(SLOTS)]
            act_out = [sb(f"d_act{s}", [P, HC, PR], c=c) for s in range(SLOTS)]
            act_hi = [sb(f"d_act_hi{s}", [P, HC, PR], F32R, c) for s in range(SLOTS)]
            act_lo = [sb(f"d_act_lo{s}", [P, HC, PR], F32R, c) for s in range(SLOTS)]
            h2 = [sb(f"d_h2{s}", [P, 2, D], c=c) for s in range(SLOTS)]
            square = [sb(f"d_square{s}", [P, 2, D], c=c) for s in range(SLOTS)]
            turned = ps("d_turned", [P, KC, PR], c)
            hidden = [ps(f"d_hidden{s}", [P, HC, PR], c) for s in range(SLOTS)]
            prod = [ps(f"d_prod{s}", [P, 2, D], c) for s in range(SLOTS)]
            ln = norm_buffers(c, "d")
            base_in = sems(c, *(f"d_base_in{s}" for s in range(SLOTS)))
            neigh_in = sems(c, *(f"d_neigh_in{s}" for s in range(SLOTS)))
            x1_stored = sems(c, *(f"d_x1_stored{s}" for s in range(SLOTS)))
            h2_stored = sems(c, *(f"d_h2_stored{s}" for s in range(SLOTS)))
            (x1_ok, h_ok, turned_ok, hi_ok, lo_ok, hidden_ok, act_ok, act_hi_ok, act_lo_ok, prod_ok, h2_ok,
             square_ok, sums_ok, cleared) = sems(c, *("d_" + name for name in (
                 "x1_ok h_ok turned_ok hi_ok lo_ok hidden_ok act_ok act_hi_ok act_lo_ok prod_ok h2_ok "
                 "square_ok sums_ok cleared").split()))
            block = c.enter_context(nc.Block())

            @block.sync
            def _(sp):
                for n, s in pair_steps(sp, 4):
                    if live(n):
                        base_source, neigh_source = node_rows(base, n), node_rows(neigh, n)
                        if late(n, SLOTS):
                            sp.wait_ge(x1_ok, n - 1)
                        sp.dma_start(node_tile(bt[s], n), base_source).then_inc(base_in[s], 16)
                        if late(n, SLOTS):
                            sp.wait_ge(h_ok, n - 1)
                        sp.dma_start(node_tile(nt[s], n), neigh_source).then_inc(neigh_in[s], 16)
                    m, q = n - 1, (s + 1) % SLOTS
                    if live(m):
                        target = node_rows(x1_rows, m)
                        sp.wait_ge(x1_ok, m + 1)
                        sp.dma_start(target, node_tile(x1[q], m)).then_inc(x1_stored[q], 16)
                    m, q = n - 4, s
                    if live(m):
                        target = node_rows(h2_rows, m)
                        sp.wait_ge(h2_ok, m + 1)
                        sp.dma_start(target, node_tile(h2[q], m)).then_inc(h2_stored[q], 16)
                for s in range(SLOTS):
                    sp.wait_ge(x1_stored[s], 16 * PAIRS // SLOTS)
                    sp.wait_ge(h2_stored[s], 16 * PAIRS // SLOTS)

            @block.tensor
            def _(pe):
                for n, s in pair_steps(pe, 2):
                    m, q = n - 1, (s + 1) % SLOTS
                    if live(m):
                        pe.wait_ge(lo_ok, m + 1)
                        if late(m, SLOTS):
                            pe.wait_ge(act_ok, m - 1)
                        for f in range(HC):
                            mm = product(pe, hidden[q][:, f, :],
                                         [(w1s[0][:, k, f * P:(f + 1) * P], w1s[1][:, k, f * P:(f + 1) * P],
                                           hi[q][:, k, :], lo[q][:, k, :]) for k in range(KC)])
                        mm.then_inc(hidden_ok, 1)
                    if live(n):
                        pe.wait_ge(h_ok, n + 1)
                        if late(n, 1):
                            pe.wait_ge(lo_ok, n)
                        for k in range(KC):
                            for r in range(2):
                                t = pe.transpose(turned[:, k, r * P:(r + 1) * P],
                                                 h[s][:, r, k * P:(k + 1) * P], ident[:, :])
                        t.then_inc(turned_ok, 1)
                    m, q = n - 2, s
                    if live(m):
                        pe.wait_ge(act_lo_ok, m + 1)
                        if late(m, SLOTS):
                            pe.wait_ge(square_ok, m - 1)
                        for r in range(2):
                            mm = product(pe, prod[q][:, r, :],
                                         [(act_hi[q][:, f, r * P:(r + 1) * P], act_lo[q][:, f, r * P:(r + 1) * P],
                                           w2s[0][:, f, :], w2s[1][:, f, :]) for f in range(HC)])
                        mm.then_inc(prod_ok, 1)

            @block.scalar
            def _(act):
                for n, s in pair_steps(act, 4):
                    m, q = n - 2, s
                    if live(m):
                        act.wait_ge(turned_ok, m + 1)
                        if late(m, SLOTS):
                            act.wait_ge(hidden_ok, m - 1)
                        act.copy(hi[q][:, :, :], turned[:, :, :]).then_inc(hi_ok, 1)
                    m, q = n - 3, (s + 1) % SLOTS
                    if live(m):
                        act.wait_ge(hidden_ok, m + 1)
                        if late(m, SLOTS):
                            act.wait_ge(act_lo_ok, m - 1)
                        for f in range(HC):
                            a = act.activation(act_out[q][:, f, :], hidden[q][:, f, :], ACT.Relu, bias=b1_col[:, f:f + 1])
                        a.then_inc(act_ok, 1)
                    m, q = n - 4, s
                    if live(m):
                        act.wait_ge(prod_ok, m + 1)
                        if late(m, SLOTS):
                            act.wait_ge(h2_stored[q], used_before(m, q))
                            act.wait_ge(sums_ok, m - 1)
                        act.copy(h2[q][:, :, :], prod[q][:, :, :]).then_inc(h2_ok, 1)
                        act.activation(square[q][:, :, :], prod[q][:, :, :], ACT.Square).then_inc(square_ok, 1)
                    if live(n):
                        norm_root(act, n, s, ln)

            @block.gpsimd
            def _(pool):
                pool.memset(h2_sum[:, :, :], 0.0).then_inc(cleared, 1)
                pool.memset(h2_squares[:, :, :], 0.0).then_inc(cleared, 1)
                pool.wait_ge(cleared, 2)
                for n, s in pair_steps(pool):
                    part = (lambda t: t[0:TAIL, 0, :]) if last(n) else (lambda t: t[:, :, :])
                    pool.wait_ge(h2_ok, n + 1)
                    pool.wait_ge(square_ok, n + 1)
                    if late(n, 1):
                        pool.wait_ge(sums_ok, n)
                    pool.tensor_tensor(part(h2_sum), part(h2_sum), part(h2[s]), ALU.add)
                    pool.tensor_tensor(part(h2_squares), part(h2_squares), part(square[s]), ALU.add).then_inc(sums_ok, 1)

            @block.vector
            def _(dve):
                for n, s in pair_steps(dve, 3):
                    m, q = n - 2, s
                    if live(m):
                        dve.wait_ge(hi_ok, m + 1)
                        dve.tensor_tensor(lo[q][:, :, :], turned[:, :, :], hi[q][:, :, :].bitcast(F32),
                                          ALU.subtract).then_inc(lo_ok, 1)
                    m, q = n - 3, (s + 1) % SLOTS
                    if live(m):
                        dve.wait_ge(act_ok, m + 1)
                        if late(m, SLOTS):
                            dve.wait_ge(prod_ok, m - 1)
                        dve.tensor_copy(act_hi[q][:, :, :], act_out[q][:, :, :]).then_inc(act_hi_ok, 1)
                        dve.wait_ge(act_hi_ok, m + 1)
                        dve.tensor_tensor(act_lo[q][:, :, :], act_out[q][:, :, :], act_hi[q][:, :, :].bitcast(F32),
                                          ALU.subtract).then_inc(act_lo_ok, 1)
                    if live(n):
                        dve.wait_ge(base_in[s], uses(n, s))
                        norm_stats(dve, n, s, ln, bt[s])
                    if live(n):
                        if late(n, SLOTS):
                            dve.wait_ge(x1_stored[s], used_before(n, s))
                        norm_apply(dve, n, s, ln, bt[s], x1[s], x1_ok)
                        dve.wait_ge(x1_ok, n + 1)
                        dve.wait_ge(neigh_in[s], uses(n, s))
                        if late(n, SLOTS):
                            dve.wait_ge(turned_ok, n - 1)
                        dve.scalar_tensor_tensor(h[s][:, :, :], x1[s][:, :, :], eps1_col[:, 0:1], nt[s][:, :, :],
                                                 ALU.mult, ALU.add).then_inc(h_ok, 1)

        bn_scale = sb("bn_scale", [P, D])
        bn_shift = sb("bn_shift", [P, D])
        with ExitStack() as c:
            gamma_b, beta_b, b2_b = (sb(name, [P, D], c=c) for name in ("gamma_b", "beta_b", "b2_b"))
            mean, second, mean_sq, var, root, rstd, mean_b2, apart, scaled = (
                sb("bn_" + name, [P, D], c=c) for name in
                "mean second mean_sq var root rstd mean_b2 apart scaled".split())
            totals = ps("bn_totals", [P, 2, D], c)
            loaded, totals_ok, var_ok, root_ok, chain = sems(c, "bn_loaded", "bn_totals_ok", "bn_var_ok", "bn_root_ok", "bn_chain")
            block = c.enter_context(nc.Block())

            @block.sync
            def _(sp):
                for tile, row in ((gamma_b, gamma), (beta_b, beta), (b2_b, b2)):
                    sp.dma_start(tile[:, :], row.rearrange("(a d) -> a d", a=1).to_broadcast([P, D])).then_inc(loaded, 16)

            @block.tensor
            def _(pe):
                for i, sums in enumerate((h2_sum, h2_squares)):
                    for r in range(2):
                        mm = pe.matmul(totals[:, i, :], ones[:, :], sums[:, r, :], start=(r == 0), stop=(r == 1))
                mm.then_inc(totals_ok, 1)

            @block.scalar
            def _(act):
                act.wait_ge(var_ok, 1)
                act.activation(root[:, :], var[:, :], ACT.Sqrt).then_inc(root_ok, 1)

            @block.vector
            def _(dve):
                dve.wait_ge(loaded, 48)
                dve.wait_ge(totals_ok, 1)
                dve.tensor_scalar(mean[:, :], totals[:, 0, :], 1.0 / N, None, ALU.mult).then_inc(chain, 1)
                dve.tensor_scalar(second[:, :], totals[:, 1, :], 1.0 / N, EPS, ALU.mult, ALU.add).then_inc(chain, 1)
                dve.wait_ge(chain, 2)
                dve.tensor_tensor(mean_sq[:, :], mean[:, :], mean[:, :], ALU.mult).then_inc(chain, 1)
                dve.tensor_tensor(mean_b2[:, :], mean[:, :], b2_b[:, :], ALU.add).then_inc(chain, 1)
                dve.wait_ge(chain, 4)
                dve.tensor_tensor(var[:, :], second[:, :], mean_sq[:, :], ALU.subtract).then_inc(var_ok, 1)
                dve.tensor_tensor(apart[:, :], b2_b[:, :], mean_b2[:, :], ALU.subtract).then_inc(chain, 1)
                dve.wait_ge(root_ok, 1)
                dve.reciprocal(rstd[:, :], root[:, :]).then_inc(chain, 1)
                dve.wait_ge(chain, 6)
                dve.tensor_tensor(bn_scale[:, :], rstd[:, :], gamma_b[:, :], ALU.mult).then_inc(chain, 1)
                dve.wait_ge(chain, 7)
                dve.tensor_tensor(scaled[:, :], apart[:, :], bn_scale[:, :], ALU.mult).then_inc(chain, 1)
                dve.wait_ge(chain, 8)
                dve.tensor_tensor(bn_shift[:, :], scaled[:, :], beta_b[:, :], ALU.add)

        with ExitStack() as c:
            x1 = [sb(f"e_x1{s}", [P, 2, D], c=c) for s in range(GATHERS)]
            h2 = [sb(f"e_h2{s}", [P, 2, D], c=c) for s in range(GATHERS)]
            shifted = [sb(f"e_shifted{s}", [P, 2, D], c=c) for s in range(GATHERS)]
            scaled = [sb(f"e_scaled{s}", [P, 2, D], c=c) for s in range(GATHERS)]
            y = [sb(f"e_y{s}", [P, 2, D], c=c) for s in range(GATHERS)]
            res = [sb(f"e_res{s}", [P, 2, D], c=c) for s in range(GATHERS)]
            stats = [sb(f"e_stats{s}", [P, 2, 6], c=c) for s in range(GATHERS)]
            mean_var = [sb(f"e_mean_var{s}", [P, 2, 2], c=c) for s in range(GATHERS)]
            root = [sb(f"e_root{s}", [P, 2], c=c) for s in range(GATHERS)]
            rstd = [sb(f"e_rstd{s}", [P, 2], c=c) for s in range(GATHERS)]
            off = [sb(f"e_off{s}", [P, 2], c=c) for s in range(GATHERS)]
            x1_in = sems(c, *(f"e_x1_in{s}" for s in range(GATHERS)))
            h2_in = sems(c, *(f"e_h2_in{s}" for s in range(GATHERS)))
            stored = sems(c, *(f"e_stored{s}" for s in range(GATHERS)))
            shifted_ok, scaled0_ok, scaled1_ok, y_ok, stats_ok, var_ok, root_ok, rstd_ok, off_ok, res_ok = sems(
                c, *("e_" + name for name in
                     "shifted_ok scaled0_ok scaled1_ok y_ok stats_ok var_ok root_ok rstd_ok off_ok res_ok".split()))
            block = c.enter_context(nc.Block())

            @block.sync
            def _(sp):
                for n, s in pair_steps(sp, 5, GATHERS):
                    if live(n):
                        x1_source, h2_source = node_rows(x1_rows, n), node_rows(h2_rows, n)
                        if late(n, GATHERS):
                            sp.wait_ge(shifted_ok, n - 3)
                        sp.dma_start(node_tile(x1[s], n), x1_source).then_inc(x1_in[s], 16)
                        if late(n, GATHERS):
                            sp.wait_ge(y_ok, n - 3)
                        sp.dma_start(node_tile(h2[s], n), h2_source).then_inc(h2_in[s], 16)
                    m, q = n - 5, (s + 3) % GATHERS
                    if live(m):
                        target = node_rows(out, m)
                        sp.wait_ge(res_ok, m + 1)
                        sp.dma_start(target, node_tile(res[q], m)).then_inc(stored[q], 16)
                for s in range(GATHERS):
                    sp.wait_ge(stored[s], 16 * PAIRS // GATHERS)

            @block.gpsimd
            def _(pool):
                for n, s in pair_steps(pool, 0, GATHERS):
                    if late(n, GATHERS):
                        pool.wait_ge(y_ok, n - 3)
                    pool.wait_ge(x1_in[s], uses(n, s, 1, GATHERS))
                    pool.tensor_tensor(shifted[s][:, :, :], x1[s][:, :, :], twice(bn_shift), ALU.add).then_inc(shifted_ok, 1)
                    pool.wait_ge(h2_in[s], uses(n, s, 1, GATHERS))
                    pool.tensor_tensor(scaled[s][:, 1, :], h2[s][:, 1, :], bn_scale[:, :], ALU.mult).then_inc(scaled1_ok, 1)

            @block.scalar
            def _(act):
                for n, s in pair_steps(act, 1, GATHERS):
                    if live(n):
                        act.wait_ge(var_ok, n + 1)
                        if late(n, GATHERS):
                            act.wait_ge(rstd_ok, n - 3)
                        act.activation(root[s][:, :], mean_var[s][:, :, 1], ACT.Sqrt, bias=eps_col[:, 0:1]).then_inc(root_ok, 1)
                    m, q = n - 1, (s + 3) % GATHERS
                    if live(m):
                        act.wait_ge(off_ok, m + 1)
                        if late(m, GATHERS):
                            act.wait_ge(stored[q], used_before(m, q, 1, GATHERS))
                        for r in range(2):
                            t = act.activation(res[q][:, r, :], y[q][:, r, :], ACT.Identity, bias=off[q][:, r:r + 1],
                                               scale=rstd[q][:, r:r + 1])
                        t.then_inc(res_ok, 1)

            @block.vector
            def _(dve):
                for n, s in pair_steps(dve, 2, GATHERS):
                    m, q = n - 1, (s + 3) % GATHERS
                    k, t = n - 2, (s + 2) % GATHERS
                    if live(n):
                        dve.wait_ge(h2_in[s], uses(n, s, 1, GATHERS))
                        dve.tensor_tensor(scaled[s][:, 0, :], h2[s][:, 0, :], bn_scale[:, :], ALU.mult).then_inc(scaled0_ok, 1)
                    if live(m):
                        dve.wait_ge(y_ok, m + 1)
                        for r in range(2):
                            last_stats = dve.bn_stats(stats[q][:, r, :], y[q][:, r, :])
                        last_stats.then_inc(stats_ok, 1)
                    if live(k):
                        dve.wait_ge(root_ok, k + 1)
                        if late(k, GATHERS):
                            dve.wait_ge(res_ok, k - 3)
                        dve.reciprocal(rstd[t][:, :], root[t][:, :]).then_inc(rstd_ok, 1)
                    if live(n):
                        dve.wait_ge(scaled0_ok, n + 1)
                        dve.wait_ge(scaled1_ok, n + 1)
                        dve.wait_ge(shifted_ok, n + 1)
                        if late(n, GATHERS):
                            dve.wait_ge(res_ok, n - 3)
                        dve.tensor_tensor(y[s][:, :, :], scaled[s][:, :, :], shifted[s][:, :, :], ALU.add).then_inc(y_ok, 1)
                    if live(k):
                        dve.wait_ge(rstd_ok, k + 1)
                        dve.scalar_tensor_tensor(off[t][:, :], mean_var[t][:, :, 0], -1.0, rstd[t][:, :],
                                                 ALU.mult, ALU.mult).then_inc(off_ok, 1)
                    if live(m):
                        dve.wait_ge(stats_ok, m + 1)
                        settle(dve)
                        for r in range(2):
                            last_var = dve.bn_aggr(mean_var[q][:, r, :], stats[q][:, r, :])
                        last_var.then_inc(var_ok, 1)


def kernel(**inputs):
    import concourse.bacc as bacc
    import numpy as np
    from concourse.bass_utils import run_bass_kernel_spmd

    nc = bacc.Bacc("TRN2", target_bir_lowering=False, num_devices=1)
    x = np.ascontiguousarray(inputs["x"])
    src, dst = np.asarray(inputs["src"]), np.asarray(inputs["dst"])
    nodes, edges = x.shape[0], src.shape[0]
    assert edges == nodes
    pairs = -(-edges // PR)
    pad = pairs * PR - edges

    def columns(a, fill):
        whole = np.concatenate([a, np.full(pad, fill, a.dtype)])
        return np.ascontiguousarray(whole.reshape(-1, P).T)

    gathers = np.stack([columns(src, 0).reshape(P, pairs, 2), columns(dst, 0).reshape(P, pairs, 2)], axis=2)
    arrays = {"x": x, "gather_cols": np.ascontiguousarray(gathers.reshape(P, -1)),
              "dst_cols": columns(dst, nodes), "dst_rows": np.concatenate([dst, np.full(pad, nodes, dst.dtype)])}
    for name in ("W_key", "W_query", "W_value", "W_skip", "bias"):
        arrays["L0_" + name] = np.ascontiguousarray(inputs["L0_gnn_" + name])
    for name in ("eps", "W1", "b1", "W2", "b2", "gamma", "beta"):
        arrays["L1_" + name] = np.ascontiguousarray(inputs["L1_gnn_" + name])
    arrays = {f"in_{name}": a for name, a in arrays.items()}
    args = [nc.dram_tensor(name, a.shape, mybir.dt.from_np(a.dtype), kind="ExternalInput").ap()
            for name, a in arrays.items()]
    args.append(nc.dram_tensor("out_rows", x.shape, F32, kind="ExternalOutput").ap())
    gnn_kernel(nc, *args)
    return run_bass_kernel_spmd(nc, [arrays], core_ids=[0]).results[0]["out_rows"]
```

```python
from contextlib import ExitStack

import concourse.bass as bass
from concourse import mybir

F32 = mybir.dt.float32
F32R = mybir.dt.float32r
I32 = mybir.dt.int32
ALU = mybir.AluOpType
ACT = mybir.ActivationFunctionType

P = 128
D = 256
KC = D // P
H = 512
HC = H // P
PR = 2 * P
SLOTS = 2
GATHERS = 4
HEAD = 8
EPS = 1e-5


def gnn_kernel(nc, x, gather_cols_in, dst_cols, dst_rows, w_key, w_query, w_value, w_skip,
               bias0, eps1, w1, b1, w2, b2, gamma, beta, out):
    N = x.shape[0]
    PAIRS = -(-N // PR)
    TAIL = N - (PAIRS - 1) * PR
    SPARE = N + 1
    ROWS = SPARE + PR
    assert TAIL <= P and dst_rows.shape[0] == PAIRS * PR

    base = nc.dram_tensor("base", (ROWS, D), F32, kind="Internal").ap()
    neigh = nc.dram_tensor("neigh", (ROWS, D), F32, kind="Internal").ap()
    x1_rows = nc.dram_tensor("x1_rows", (N, D), F32, kind="Internal").ap()
    h2_rows = nc.dram_tensor("h2_rows", (N, D), F32, kind="Internal").ap()

    def pair_steps(eng, lag=0, slots=SLOTS):
        loop_end = HEAD + (PAIRS - 1 - HEAD) // slots * slots
        for n in range(HEAD):
            yield n, n % slots
        with eng.Fori(HEAD, loop_end, slots) as i:
            for s in range(slots):
                yield i + s, s
        for n in range(loop_end, PAIRS + lag):
            yield n, n % slots

    def live(n):
        return not isinstance(n, int) or 0 <= n < PAIRS

    EDGE_LAG, NODE_LAG = 6, 5
    SCATTER_LAG = 7
    EDGE_HEAD = 12
    LEAST = EDGE_HEAD + GATHERS
    EDGE_LOOP_END = (PAIRS - 1) // GATHERS * GATHERS
    NODE_LOOP_END = (PAIRS - 1) // SLOTS * SLOTS
    TOGETHER_LAST = PAIRS + EDGE_LAG - EDGE_LOOP_END
    assert TOGETHER_LAST % SLOTS == 0 and PAIRS % 2 == 0 and PAIRS // 2 <= P

    def late(n, k):
        return not isinstance(n, int) or n >= k

    def uses(n, s, dmas=1, slots=SLOTS):
        return (n - s) * (16 * dmas // slots) + 16 * dmas

    def used_before(n, s, dmas=1, slots=SLOTS):
        return (n - s) * (16 * dmas // slots)

    def last(n):
        return isinstance(n, int) and n == PAIRS - 1

    def node_rows(table, n):
        if last(n):
            return table[n * PR:n * PR + TAIL, :]
        return table[bass.ds(n * PR, PR), :].rearrange("(p r) d -> p r d", r=2)

    def node_tile(tile, n):
        return tile[0:TAIL, 0, :] if last(n) else tile[:, :, :]

    with ExitStack() as ctx:
        def sb(name, shape, dt=F32, c=ctx):
            return c.enter_context(nc.sbuf_tensor(name, shape, dt))

        def sems(c, *names):
            return [c.enter_context(nc.semaphore(name)) for name in names]

        def twice(row):
            return row[:, :].rearrange("p (a d) -> p a d", a=1).to_broadcast([P, 2, D])

        def ps(name, shape, c):
            return c.enter_context(nc.psum_tensor(name, shape, F32))

        def product(pe, target, terms, start=True, stop=True):
            for n, (a_hi, a_lo, b_hi, b_lo) in enumerate(terms):
                pe.matmul(target, a_hi, b_hi, start=(start and n == 0), stop=False)
                pe.matmul(target, a_hi, b_lo, start=False, stop=False)
                mm = pe.matmul(target, a_lo, b_hi, start=False, stop=(stop and n == len(terms) - 1))
            return mm

        def equal_edges(dve, m, dst_row, same, row_in, row_count, same_ok, summed_ok):
            dve.wait_ge(row_in, row_count)
            if late(m, SLOTS):
                dve.wait_ge(summed_ok, m - 1)
            for j in range(2):
                eq = dve.tensor_scalar(same[:, j, :], dst_row[:, :], dst_f[:, bass.ds(2 * m + j, 1)], None, ALU.is_equal)
            eq.then_inc(same_ok, 1)

        def settle(eng):
            eng.sem_inc(settled, 1)

        def norm_buffers(c, stage):
            return ([sb(f"{stage}_stats{s}", [P, 2, 6], c=c) for s in range(SLOTS)],
                    [sb(f"{stage}_mean_var{s}", [P, 2, 2], c=c) for s in range(SLOTS)],
                    [sb(f"{stage}_root{s}", [P, 2], c=c) for s in range(SLOTS)],
                    [sb(f"{stage}_rstd{s}", [P, 2], c=c) for s in range(SLOTS)],
                    *sems(c, f"{stage}_stats_ok", f"{stage}_var_ok", f"{stage}_root_ok", f"{stage}_rstd_ok"))

        def norm_stats(dve, n, s, ln, rows):
            stats, mean_var, root, rstd, stats_ok, var_ok, root_ok, rstd_ok = ln
            for r in range(2):
                t = dve.bn_stats(stats[s][:, r, :], rows[:, r, :])
            t.then_inc(stats_ok, 1)

        def norm_var(dve, n, s, ln):
            stats, mean_var, root, rstd, stats_ok, var_ok, root_ok, rstd_ok = ln
            dve.wait_ge(stats_ok, n + 1)
            settle(dve)
            for r in range(2):
                t = dve.bn_aggr(mean_var[s][:, r, :], stats[s][:, r, :])
            t.then_inc(var_ok, 1)

        def norm_root(act, n, s, ln):
            stats, mean_var, root, rstd, stats_ok, var_ok, root_ok, rstd_ok = ln
            act.wait_ge(var_ok, n + 1)
            act.activation(root[s][:, :], mean_var[s][:, :, 1], ACT.Sqrt, bias=eps_col[:, 0:1]).then_inc(root_ok, 1)

        def norm_rstd(dve, n, s, ln):
            stats, mean_var, root, rstd, stats_ok, var_ok, root_ok, rstd_ok = ln
            dve.wait_ge(root_ok, n + 1)
            dve.reciprocal(rstd[s][:, :], root[s][:, :]).then_inc(rstd_ok, 1)

        def norm_apply(dve, n, s, ln, rows, target, target_ok):
            stats, mean_var, root, rstd, stats_ok, var_ok, root_ok, rstd_ok = ln
            dve.wait_ge(rstd_ok, n + 1)
            for r in range(2):
                t = dve.tensor_scalar(target[:, r, :], rows[:, r, :], mean_var[s][:, r, 0:1], rstd[s][:, r:r + 1],
                                      ALU.subtract, ALU.mult)
            t.then_inc(target_ok, 1)

        [settled] = sems(ctx, "settled")

        ident = sb("ident", [P, P])
        ones = sb("ones", [P, P])
        wqv = [sb(f"wqv_{q}", [P, KC, 2 * D], F32R) for q in ("hi", "lo")]
        wk = [sb(f"wk_{q}", [P, KC, D], F32R) for q in ("hi", "lo")]
        ws = [sb(f"ws_{q}", [P, KC, D], F32R) for q in ("hi", "lo")]
        w1s = [sb(f"w1_{q}", [P, KC, H], F32R) for q in ("hi", "lo")]
        w2s = [sb(f"w2_{q}", [P, HC, D], F32R) for q in ("hi", "lo")]
        bias0_b = sb("bias0_b", [P, D])
        b1_col = sb("b1_col", [P, HC])
        eps1_col = sb("eps1_col", [P, 1])
        eps_col = sb("eps_col", [P, 1])
        gather_cols = sb("gather_cols", [P, 4 * PAIRS], I32)
        dst_f = sb("dst_f", [P, 2 * PAIRS])
        scatter_i = sb("scatter_i", [P, 2 * PAIRS], I32)
        earlier = sb("earlier", [P, 2, PR])
        spare_f = sb("spare_f", [P, 2])
        zero = sb("zero", [P, 2, D])
        plan = sb("plan", [1, 6], I32)

        with ExitStack() as c:
            raw = sb("raw_w", [P, 4, 2 * D * KC], c=c)
            spare_i = sb("spare_i", [P, 2], I32, c)
            eps_raw = sb("eps_raw", [P, 1], c=c)
            dst_i = sb("dst_i", [P, 2 * PAIRS], I32, c)
            loaded, made, zero_made, split_hi, zeroed = sems(c, "loaded", "made", "zero_made", "split_hi", "zeroed")
            raw_v = raw[:, :, :]

            def raw_part(k, width, cols):
                return raw_v[:, k, :].rearrange("p (c n) -> p c n", n=width)[:, :, cols[0]:cols[1]]

            block = c.enter_context(nc.Block())

            @block.sync
            def _(sp):
                for k, width, cols, w in ((0, 2 * D, (0, D), w_query), (0, 2 * D, (D, 2 * D), w_value),
                                          (1, 2 * D, (0, D), w_key), (1, 2 * D, (D, 2 * D), w_skip),
                                          (2, H, (0, H), w1), (3, D, (0, D), w2)):
                    sp.dma_start(raw_part(k, width, cols), w.rearrange("(c p) n -> p c n", p=P)).then_inc(loaded, 16)
                for tile, array in ((bias0_b, bias0.rearrange("(a d) -> a d", a=1).to_broadcast([P, D])),
                                    (eps_raw, eps1.rearrange("(a d) -> a d", a=1).to_broadcast([P, 1])),
                                    (gather_cols, gather_cols_in), (dst_i, dst_cols)):
                    sp.dma_start(tile[:, :], array).then_inc(loaded, 16)
                with nc.allow_non_contiguous_dma(reason="512 biases, once"):
                    sp.dma_start(b1_col[:, :], b1.rearrange("(c p) -> p c", p=P)).then_inc(loaded, 16)
                sp.wait_ge(zero_made, 1)
                for first in range(N, ROWS, P):
                    count = min(P, ROWS - first)
                    sp.dma_start(base[first:first + count, :], zero[0:count, 0, :]).then_inc(zeroed, 16)
                sp.wait_ge(zeroed, 16 * -((N - ROWS) // P))

            @block.gpsimd
            def _(pool):
                pool.memset(ident[:, :], 0.0).then_inc(made, 1)
                pool.memset(ones[:, :], 1.0).then_inc(made, 1)
                pool.memset(earlier[:, :, :], 1.0).then_inc(made, 1)
                pool.wait_ge(made, 3)
                pool.affine_select(out=ident[:, :], in_=ident[:, :], compare_op=ALU.not_equal, fill=1.0, base=0,
                                   pattern=[[-1, P]], channel_multiplier=1).then_inc(made, 1)
                for t in range(2):
                    pool.affine_select(out=earlier[:, t, :], in_=earlier[:, t, :], compare_op=ALU.is_gt, fill=0.0,
                                       base=t * P, pattern=[[-1, PR]], channel_multiplier=1).then_inc(made, 1)
                pool.iota(spare_i[:, :], pattern=[[P, 2]], base=SPARE, channel_multiplier=1).then_inc(made, 1)

            @block.vector
            def _(dve):
                dve.memset(zero[:, :, :], 0.0).then_inc(zero_made, 1)
                dve.wait_ge(loaded, 16 * 11)
                parts = ((0, 2 * D, (0, 2 * D), wqv), (1, 2 * D, (0, D), wk), (1, 2 * D, (D, 2 * D), ws),
                         (2, H, (0, H), w1s), (3, D, (0, D), w2s))
                for k, width, cols, (hi, lo) in parts:
                    dve.tensor_copy(hi[:, :, :], raw_part(k, width, cols)).then_inc(split_hi, 1)
                for n, (k, width, cols, (hi, lo)) in enumerate(parts):
                    dve.wait_ge(split_hi, n + 1)
                    dve.tensor_tensor(lo[:, :, :], raw_part(k, width, cols), hi[:, :, :].bitcast(F32), ALU.subtract)
                dve.tensor_copy(dst_f[:, :], dst_i[:, :])
                dve.tensor_scalar(eps1_col[:, :], eps_raw[:, :], 1.0, None, ALU.add)
                dve.memset(eps_col[:, :], EPS)
                dve.wait_ge(made, 7)
                dve.tensor_copy(spare_f[:, :], spare_i[:, :])

        with ExitStack() as c:
            all_i = sb("plan_all_i", [PAIRS // 2, 2, PR], I32, c)
            first_i = sb("plan_first_i", [PAIRS // 2, 2], I32, c)
            all_f = sb("plan_all_f", [PAIRS // 2, 2, PR], c=c)
            first_f, min_dst, asked = (sb("plan_" + name, [PAIRS // 2, 2], c=c) for name in ("first_f", "min_dst", "asked"))
            across = sb("plan_across", [PAIRS // 2, 1], c=c)
            names = "most at_least whole offset0 gap jump offset lead longer".split()
            most, at_least, whole, offset0, gap, jump, offset, lead, longer = (
                sb("plan_" + name, [1, 1], c=c) for name in names)
            whole_i = sb("plan_whole_i", [1, 1], I32, c)
            plan_f = sb("plan_f", [1, 6], c=c)
            line = ps("plan_line", [1, P], c)
            loaded, numbered, across_ok, line_ok, chain = sems(
                c, *("plan_" + name for name in "loaded numbered across_ok line_ok chain".split()))
            block = c.enter_context(nc.Block())

            @block.sync
            def _(sp):
                sp.dma_start(all_i[:, :, :], dst_rows.rearrange("(p r e) -> p r e", r=2, e=PR)).then_inc(loaded, 16)

            @block.gpsimd
            def _(pool):
                pool.iota(first_i[:, :], pattern=[[PR, 2]], base=PR * (SCATTER_LAG + 1),
                          channel_multiplier=2 * PR).then_inc(numbered, 1)

            @block.tensor
            def _(pe):
                pe.wait_ge(across_ok, 1)
                pe.transpose(line[0:1, 0:PAIRS // 2], across[:, :], ident[0:PAIRS // 2, 0:PAIRS // 2]).then_inc(line_ok, 1)

            @block.vector
            def _(dve):
                steps = 0

                def then(instruction):
                    nonlocal steps
                    steps += 1
                    instruction.then_inc(chain, 1)
                    dve.wait_ge(chain, steps)

                dve.wait_ge(numbered, 1)
                dve.tensor_copy(first_f[:, :], first_i[:, :])
                dve.wait_ge(loaded, 16)
                then(dve.tensor_copy(all_f[:, :, :], all_i[:, :, :]))
                then(dve.tensor_reduce(min_dst[:, :], all_f[:, :, :], mybir.AxisListType.X, ALU.min))
                then(dve.tensor_tensor(asked[:, :], first_f[:, :], min_dst[:, :], ALU.subtract))
                dve.tensor_reduce(across[:, :], asked[:, :], mybir.AxisListType.X, ALU.max).then_inc(across_ok, 1)
                dve.wait_ge(line_ok, 1)
                then(dve.tensor_reduce(most[:, :], line[:, 0:PAIRS // 2], mybir.AxisListType.X, ALU.max))
                then(dve.tensor_scalar(at_least[:, :], most[:, :], float(LEAST * PR), 1.0 / (GATHERS * PR), ALU.max, ALU.mult))
                then(dve.tensor_scalar(whole_i[:, :], at_least[:, :], 1.0, None, ALU.add))
                then(dve.tensor_copy(whole[:, :], whole_i[:, :]))
                then(dve.tensor_scalar(offset0[:, :], whole[:, :], float(GATHERS), None, ALU.mult))
                then(dve.tensor_scalar(gap[:, :], offset0[:, :], -1.0, float(EDGE_LOOP_END), ALU.mult, ALU.add))
                then(dve.scalar_tensor_tensor(jump[:, :], offset0[:, :], float(EDGE_LOOP_END - LEAST), gap[:, :],
                                              ALU.is_gt, ALU.mult))
                then(dve.tensor_tensor(offset[:, :], offset0[:, :], jump[:, :], ALU.add))
                then(dve.tensor_scalar(lead[:, :], offset[:, :], -1.0, float(EDGE_LOOP_END), ALU.mult, ALU.add))
                then(dve.tensor_scalar(longer[:, :], lead[:, :], float(TOGETHER_LAST - HEAD), None, ALU.add))
                dve.tensor_copy(plan_f[:, 0:1], offset[:, :])
                dve.tensor_scalar(plan_f[:, 1:2], offset[:, :], float(-LEAST), None, ALU.add)
                dve.tensor_copy(plan_f[:, 2:3], lead[:, :])
                dve.tensor_scalar(plan_f[:, 3:4], lead[:, :], float(-LEAST), 0.0, ALU.add, ALU.max)
                then(dve.scalar_tensor_tensor(plan_f[:, 4:5], lead[:, :], 0.0, longer[:, :], ALU.is_gt, ALU.mult))
                then(dve.tensor_scalar(plan_f[:, 5:6], plan_f[:, 4:5], -1.0, float(NODE_LOOP_END), ALU.mult, ALU.add))
                dve.tensor_copy(plan[:, :], plan_f[:, :])

        with ExitStack() as c:
            xt = [sb(f"a_x{s}", [P, 2, D], c=c) for s in range(GATHERS)]
            xb = [sb(f"a_xb{s}", [P, 2, D], c=c) for s in range(GATHERS)]
            res = [sb(f"a_res{s}", [P, 2, D], c=c) for s in range(GATHERS)]
            hi = [sb(f"a_hi{s}", [P, KC, PR], F32R, c) for s in range(GATHERS)]
            lo = [sb(f"a_lo{s}", [P, KC, PR], F32R, c) for s in range(GATHERS)]
            turned = [ps(f"a_turned{s}", [P, KC, PR], c) for s in range(SLOTS)]
            prod = [ps(f"a_prod{s}", [P, 2, D], c) for s in range(SLOTS)]
            x_in = sems(c, *(f"a_x_in{s}" for s in range(GATHERS)))
            stored = sems(c, *(f"a_stored{s}" for s in range(GATHERS)))
            turned_ok, hi_ok, lo_ok, prod_ok, xb_ok, res_ok = sems(
                c, "a_turned_ok", "a_hi_ok", "a_lo_ok", "a_prod_ok", "a_xb_ok", "a_res_ok")
            block = c.enter_context(nc.Block())

            @block.sync
            def _(sp):
                for n, g in pair_steps(sp, 5, GATHERS):
                    if live(n):
                        source = node_rows(x, n)
                        if late(n, GATHERS):
                            sp.wait_ge(turned_ok, n - 3)
                            sp.wait_ge(xb_ok, n - 3)
                        sp.dma_start(node_tile(xt[g], n), source).then_inc(x_in[g], 16)
                    m, q = n - 5, (g + 3) % GATHERS
                    if live(m):
                        target = node_rows(base, m)
                        sp.wait_ge(res_ok, m + 1)
                        sp.dma_start(target, node_tile(res[q], m)).then_inc(stored[q], 16)
                for s in range(GATHERS):
                    sp.wait_ge(stored[s], 16 * PAIRS // GATHERS)

            @block.tensor
            def _(pe):
                for n, g in pair_steps(pe, 2, GATHERS):
                    s = g % SLOTS
                    if live(n):
                        pe.wait_ge(x_in[g], uses(n, g, 1, GATHERS))
                        if late(n, SLOTS):
                            pe.wait_ge(lo_ok, n - 1)
                        for k in range(KC):
                            for r in range(2):
                                t = pe.transpose(turned[s][:, k, r * P:(r + 1) * P],
                                                 xt[g][:, r, k * P:(k + 1) * P], ident[:, :])
                        t.then_inc(turned_ok, 1)
                    m, q, g = n - 2, s, (g + 2) % GATHERS
                    if live(m):
                        pe.wait_ge(lo_ok, m + 1)
                        if late(m, SLOTS):
                            pe.wait_ge(res_ok, m - 1)
                        for r in range(2):
                            mm = product(pe, prod[q][:, r, :],
                                         [(hi[g][:, k, r * P:(r + 1) * P], lo[g][:, k, r * P:(r + 1) * P],
                                           ws[0][:, k, :], ws[1][:, k, :]) for k in range(KC)])
                        mm.then_inc(prod_ok, 1)

            @block.scalar
            def _(act):
                for n, g in pair_steps(act, 0, GATHERS):
                    act.wait_ge(turned_ok, n + 1)
                    if late(n, GATHERS):
                        act.wait_ge(prod_ok, n - 3)
                    act.copy(hi[g][:, :, :], turned[g % SLOTS][:, :, :]).then_inc(hi_ok, 1)

            @block.gpsimd
            def _(pool):
                for n, g in pair_steps(pool, 0, GATHERS):
                    pool.wait_ge(x_in[g], uses(n, g, 1, GATHERS))
                    if late(n, GATHERS):
                        pool.wait_ge(res_ok, n - 3)
                    pool.tensor_tensor(xb[g][:, :, :], xt[g][:, :, :], twice(bias0_b), ALU.add).then_inc(xb_ok, 1)

            @block.vector
            def _(dve):
                for n, g in pair_steps(dve, 3, GATHERS):
                    m, q = n - 3, (g + 1) % GATHERS
                    if live(m):
                        dve.wait_ge(prod_ok, m + 1)
                        dve.wait_ge(xb_ok, m + 1)
                        if late(m, GATHERS):
                            dve.wait_ge(stored[q], used_before(m, q, 1, GATHERS))
                        dve.tensor_tensor(res[q][:, :, :], prod[q % SLOTS][:, :, :], xb[q][:, :, :], ALU.add).then_inc(res_ok, 1)
                    if live(n):
                        dve.wait_ge(hi_ok, n + 1)
                        dve.tensor_tensor(lo[g][:, :, :], turned[g % SLOTS][:, :, :], hi[g][:, :, :].bitcast(F32),
                                          ALU.subtract).then_inc(lo_ok, 1)

        with ExitStack() as c:
            gather_i = [sb(f"b_gather_i{s}", [P, 2, 2], I32, c) for s in range(GATHERS)]
            xe = [sb(f"b_x{s}", [P, 2, 2, D], c=c) for s in range(GATHERS)]
            dst_row = [sb(f"b_dst_row{s}", [P, PR], I32, c) for s in range(SLOTS)]
            same = [sb(f"b_same{s}", [P, 2, PR], F32R, c) for s in range(SLOTS)]
            marked = sb("b_marked", [P, 2, PR], c=c)
            count = sb("b_count", [P, 2], c=c)
            to_spare = sb("b_to_spare", [P, 2], c=c)
            step = sb("b_step", [P, 2], c=c)
            scatter_slot = [sb(f"b_scatter_i{s}", [P, 2], I32, c) for s in range(GATHERS)]
            hi = [sb(f"b_hi{j}", [P, 2 * KC, P], F32R, c) for j in range(2)]
            lo = [sb(f"b_lo{j}", [P, 2 * KC, P], F32R, c) for j in range(2)]
            gate = [sb(f"b_gate{j}", [P, D], c=c) for j in range(2)]
            msg = [sb(f"b_msg{s}", [P, 2, D], c=c) for s in range(SLOTS)]
            msg_hi = [sb(f"b_msg_hi{s}", [P, 2, D], F32R, c) for s in range(SLOTS)]
            msg_lo = [sb(f"b_msg_lo{s}", [P, 2, D], F32R, c) for s in range(SLOTS)]
            rows = [sb(f"b_rows{s}", [P, 2, D], c=c) for s in range(GATHERS)]
            turned = [ps(f"b_turned{j}", [P, 2 * KC, P], c) for j in range(2)]
            prod = [[ps(f"b_prod{s}{j}", [P, 2 * D], c) for j in range(2)] for s in range(SLOTS)]
            summed = [ps(f"b_summed{s}", [P, 2, D], c) for s in range(SLOTS)]
            x_in = sems(c, *(f"b_x_in{s}" for s in range(GATHERS)))
            row_in = sems(c, *(f"b_row_in{s}" for s in range(SLOTS)))
            (zeroed, msg_hi_ok, msg_lo_ok, gather_i_ok, turned_ok, hi_ok, lo_ok, prod_ok, gate_ok, msg_ok, same_ok, marked_ok, index_ok,
             index_step, summed_ok, rows_ok, scattered) = sems(
                c, *("b_" + name for name in (
                    "zeroed msg_hi_ok msg_lo_ok gather_i_ok turned_ok hi_ok lo_ok prod_ok gate_ok msg_ok same_ok marked_ok index_ok "
                    "index_step summed_ok rows_ok scattered").split()))
            block = c.enter_context(nc.Block())

            @block.sync
            def _(sp):
                for n, s in pair_steps(sp):
                    source = dst_rows[bass.ds(n * PR, PR)].rearrange("(a e) -> a e", a=1).to_broadcast([P, PR])
                    if late(n, SLOTS):
                        sp.wait_ge(same_ok, n - 1)
                    sp.dma_start(dst_row[s][:, :], source).then_inc(row_in[s], 16)
                    first = PAIRS * PR if last(n) else n * PR
                    if last(n):
                        sp.dma_start(neigh[n * PR:(n + 1) * PR, :].rearrange("(p r) d -> p r d", r=2),
                                     zero[:, :, :]).then_inc(zeroed, 16)
                        sp.dma_start(neigh[first:ROWS, :], zero[0:ROWS - first, 0, :]).then_inc(zeroed, 16)
                    else:
                        sp.dma_start(neigh[bass.ds(first, PR), :].rearrange("(p r) d -> p r d", r=2),
                                     zero[:, :, :]).then_inc(zeroed, 16)
                sp.wait_ge(zeroed, 16 * (PAIRS + 1))

            @block.gpsimd
            def _(pool):
                for n, s in pair_steps(pool, 5, GATHERS):
                    if live(n):
                        pool.wait_ge(gather_i_ok, n + 1)
                        if late(n, GATHERS):
                            pool.wait_ge(turned_ok, 2 * n - 6)
                        settle(pool)
                        for e in range(2):
                            for j in range(2):
                                pool.indirect_dma_start(
                                    out=xe[s][:, e, j, :], out_offset=None, in_=x,
                                    in_offset=bass.IndirectOffsetOnAxis(ap=gather_i[s][:, e, j:j + 1], axis=0),
                                ).then_inc(x_in[s], 16)
                    m, q = n - 5, (s + 3) % GATHERS
                    if live(m):
                        pool.wait_ge(rows_ok, m + 1)
                        pool.wait_ge(index_ok, m + 1)
                        if late(m, 1):
                            pool.wait_ge(scattered, 32 * m)
                        settle(pool)
                        for j in range(2):
                            pool.indirect_dma_start(
                                out=base, out_offset=bass.IndirectOffsetOnAxis(ap=scatter_slot[q][:, j:j + 1], axis=0),
                                in_=rows[q][:, j, :], in_offset=None, compute_op=ALU.add).then_inc(scattered, 16)
                pool.wait_ge(scattered, 32 * PAIRS)

            @block.tensor
            def _(pe):
                for n, g in pair_steps(pe, 2, GATHERS):
                    if live(n):
                        pe.wait_ge(x_in[g], uses(n, g, 4, GATHERS))
                        for j in range(2):
                            if late(n, 1):
                                pe.wait_ge(lo_ok, 2 * n + j - 1)
                            for e in range(2):
                                for k in range(KC):
                                    t = pe.transpose(turned[j][:, e * KC + k, :],
                                                     xe[g][:, e, j, k * P:(k + 1) * P], ident[:, :])
                            t.then_inc(turned_ok, 1)
                    m, q = n - 1, (g + 1) % SLOTS
                    if live(m):
                        for j in range(2):
                            pe.wait_ge(lo_ok, 2 * m + j + 1)
                            if late(m, SLOTS):
                                pe.wait_ge(msg_ok, 2 * m + j - 3)
                            product(pe, prod[q][j][:, :],
                                    [(hi[j][:, k, :], lo[j][:, k, :], wqv[0][:, k, :], wqv[1][:, k, :])
                                     for k in range(KC)], stop=False)
                            mm = product(pe, prod[q][j][:, 0:D],
                                         [(hi[j][:, KC + k, :], lo[j][:, KC + k, :], wk[0][:, k, :], wk[1][:, k, :])
                                          for k in range(KC)], start=False)
                            mm.then_inc(prod_ok, 1)
                    m, q = n - 2, g % SLOTS
                    if live(m):
                        pe.wait_ge(msg_lo_ok, m + 1)
                        pe.wait_ge(same_ok, m + 1)
                        if late(m, SLOTS):
                            pe.wait_ge(rows_ok, m - 1)
                        for i in range(2):
                            for j in range(2):
                                pe.matmul(summed[q][:, i, :], same[q][:, j, i * P:(i + 1) * P], msg_hi[q][:, j, :],
                                          start=(j == 0), stop=False)
                                mm = pe.matmul(summed[q][:, i, :], same[q][:, j, i * P:(i + 1) * P], msg_lo[q][:, j, :],
                                               start=False, stop=(j == 1))
                        mm.then_inc(summed_ok, 1)

            @block.scalar
            def _(act):
                for n, s in pair_steps(act, 2, GATHERS):
                    m, q = n - 1, (s + 1) % SLOTS
                    for j in range(2):
                        if live(n):
                            act.wait_ge(turned_ok, 2 * n + j + 1)
                            if late(n, 1):
                                act.wait_ge(prod_ok, 2 * n + j - 1)
                            act.copy(hi[j][:, :, :], turned[j][:, :, :]).then_inc(hi_ok, 1)
                        if live(m):
                            act.wait_ge(prod_ok, 2 * m + j + 1)
                            if late(m, 1):
                                act.wait_ge(msg_ok, 2 * m + j - 1)
                            act.activation(gate[j][:, :], prod[q][j][:, 0:D], ACT.Sigmoid).then_inc(gate_ok, 1)
                    if live(m):
                        if late(m, SLOTS):
                            act.wait_ge(summed_ok, m - 1)
                        act.wait_ge(msg_ok, 2 * m + 2)
                        act.copy(msg_hi[q][:, :, :], msg[q][:, :, :]).then_inc(msg_hi_ok, 1)
                    m, q = n - 2, (s + 2) % GATHERS
                    if live(m):
                        act.wait_ge(summed_ok, m + 1)
                        if late(m, GATHERS):
                            act.wait_ge(scattered, 32 * (m - 3))
                        act.copy(rows[q][:, :, :], summed[q % SLOTS][:, :, :]).then_inc(rows_ok, 1)

            @block.vector
            def _(dve):
                for n, g in pair_steps(dve, 4, GATHERS):
                    if live(n):
                        if late(n, GATHERS):
                            dve.wait_ge(x_in[g], used_before(n, g, 4, GATHERS))
                        dve.tensor_copy(gather_i[g][:, :, :].rearrange("p e j -> p (e j)"),
                                        gather_cols[:, bass.ds(4 * n, 4)]).then_inc(gather_i_ok, 1)
                    ahead, m, q = n - 3, n - 4, g % SLOTS
                    for j in range(2):
                        if live(ahead):
                            dve.wait_ge(hi_ok, 2 * ahead + j + 1)
                            dve.tensor_tensor(lo[j][:, :, :], turned[j][:, :, :], hi[j][:, :, :].bitcast(F32),
                                              ALU.subtract).then_inc(lo_ok, 1)
                        if live(m):
                            dve.wait_ge(gate_ok, 2 * m + j + 1)
                            if late(m, SLOTS):
                                dve.wait_ge(msg_lo_ok, m - 1)
                            dve.tensor_tensor(msg[q][:, j, :], gate[j][:, :], prod[q][j][:, D:2 * D],
                                              ALU.mult).then_inc(msg_ok, 1)
                    if live(m):
                        equal_edges(dve, m, dst_row[q], same[q], row_in[q], uses(m, q), same_ok, summed_ok)
                        dve.wait_ge(same_ok, m + 1)
                        if late(m, 1):
                            dve.wait_ge(index_ok, m)
                        for j in range(2):
                            mark = dve.tensor_tensor_reduce(marked[:, j, :], same[q][:, j, :].bitcast(F32), earlier[:, j, :], 1.0, 0.0,
                                                            ALU.mult, ALU.add, count[:, j:j + 1])
                        mark.then_inc(index_step, 1)
                        dve.tensor_tensor(to_spare[:, :], spare_f[:, :], dst_f[:, bass.ds(2 * m, 2)],
                                          ALU.subtract).then_inc(index_step, 1)
                        dve.wait_ge(index_step, 3 * m + 2)
                        dve.scalar_tensor_tensor(step[:, :], count[:, :], 0.0, to_spare[:, :], ALU.is_gt,
                                                 ALU.mult).then_inc(index_step, 1)
                        dve.wait_ge(index_step, 3 * m + 3)
                        if late(m, GATHERS):
                            dve.wait_ge(scattered, 32 * (m - 3))
                        dve.tensor_tensor(scatter_i[:, bass.ds(2 * m, 2)], step[:, :], dst_f[:, bass.ds(2 * m, 2)], ALU.add)
                        dve.tensor_tensor(scatter_slot[g][:, :], step[:, :], dst_f[:, bass.ds(2 * m, 2)],
                                          ALU.add).then_inc(index_ok, 1)
                        dve.wait_ge(msg_hi_ok, m + 1)
                        dve.tensor_tensor(msg_lo[q][:, :, :], msg[q][:, :, :], msg_hi[q][:, :, :].bitcast(F32),
                                          ALU.subtract).then_inc(msg_lo_ok, 1)

        h2_sum = sb("h2_sum", [P, 2, D])
        h2_squares = sb("h2_squares", [P, 2, D])
        with ExitStack() as c:
            gather_i = [sb(f"c_gather_i{s}", [P, 2], I32, c) for s in range(GATHERS)]
            scatter_slot = [sb(f"c_scatter_i{s}", [P, 2], I32, c) for s in range(GATHERS)]
            xe = [sb(f"c_x{s}", [P, 2, D], c=c) for s in range(GATHERS)]
            dst_row = [sb(f"c_dst_row{s}", [P, PR], I32, c) for s in range(GATHERS)]
            same = [sb(f"c_same{s}", [P, 2, PR], F32R, c) for s in range(SLOTS)]
            normed = [sb(f"c_normed{s}", [P, 2, D], c=c) for s in range(SLOTS)]
            normed_hi = [sb(f"c_normed_hi{s}", [P, 2, D], F32R, c) for s in range(SLOTS)]
            normed_lo = [sb(f"c_normed_lo{s}", [P, 2, D], F32R, c) for s in range(SLOTS)]
            rows = [sb(f"c_rows{s}", [P, 2, D], c=c) for s in range(GATHERS)]
            summed = ps("c_summed", [P, 2, D], c)
            edge_ln = norm_buffers(c, "c")
            x_in = sems(c, *(f"c_x_in{s}" for s in range(GATHERS)))
            row_in = sems(c, *(f"c_row_in{s}" for s in range(GATHERS)))
            (gather_i_ok, same_ok, index_ok, normed_ok, normed_hi_ok, normed_lo_ok, summed_ok, rows_ok,
             scattered) = sems(
                c, *("c_" + name for name in (
                    "gather_i_ok same_ok index_ok normed_ok normed_hi_ok normed_lo_ok summed_ok rows_ok "
                    "scattered").split()))

            bt = [sb(f"d_base{s}", [P, 2, D], c=c) for s in range(SLOTS)]
            nt = [sb(f"d_neigh{s}", [P, 2, D], c=c) for s in range(SLOTS)]
            x1 = [sb(f"d_x1{s}", [P, 2, D], c=c) for s in range(SLOTS)]
            h = [sb(f"d_h{s}", [P, 2, D], c=c) for s in range(SLOTS)]
            hi = [sb(f"d_hi{s}", [P, KC, PR], F32R, c) for s in range(SLOTS)]
            lo = [sb(f"d_lo{s}", [P, KC, PR], F32R, c) for s in range(SLOTS)]
            act_out = [sb(f"d_act{s}", [P, HC, PR], c=c) for s in range(SLOTS)]
            act_hi = [sb(f"d_act_hi{s}", [P, HC, PR], F32R, c) for s in range(SLOTS)]
            act_lo = [sb(f"d_act_lo{s}", [P, HC, PR], F32R, c) for s in range(SLOTS)]
            h2 = [sb(f"d_h2{s}", [P, 2, D], c=c) for s in range(SLOTS)]
            square = [sb(f"d_square{s}", [P, 2, D], c=c) for s in range(SLOTS)]
            turned = ps("d_turned", [P, KC, PR], c)
            hidden = [ps(f"d_hidden{s}", [P, HC, PR], c) for s in range(SLOTS)]
            prod = [ps(f"d_prod{s}", [P, 2, D], c) for s in range(SLOTS)]
            node_ln = norm_buffers(c, "d")
            base_in = sems(c, *(f"d_base_in{s}" for s in range(SLOTS)))
            neigh_in = sems(c, *(f"d_neigh_in{s}" for s in range(SLOTS)))
            x1_stored = sems(c, *(f"d_x1_stored{s}" for s in range(SLOTS)))
            h2_stored = sems(c, *(f"d_h2_stored{s}" for s in range(SLOTS)))
            (x1_ok, h_ok, turned_ok, hi_ok, lo_ok, hidden_ok, act_ok, act_hi_ok, act_lo_ok, prod_ok, h2_ok,
             square_ok, sums_ok, cleared) = sems(c, *("d_" + name for name in (
                 "x1_ok h_ok turned_ok hi_ok lo_ok hidden_ok act_ok act_hi_ok act_lo_ok prod_ok h2_ok "
                 "square_ok sums_ok cleared").split()))

            def edge_and_node_steps(eng):
                offset, offset_beyond, lead, lead_beyond, rest, rest_end = (
                    eng.value_load(plan[0:1, i:i + 1], min_val=least, max_val=most) for i, (least, most) in enumerate((
                        (LEAST, EDGE_LOOP_END), (0, EDGE_LOOP_END - LEAST), (0, EDGE_LOOP_END - LEAST),
                        (0, EDGE_LOOP_END - 2 * LEAST), (0, NODE_LOOP_END - LEAST), (LEAST, NODE_LOOP_END))))
                everything = 32 * PAIRS

                def pair(number, least, most):
                    return nc.s_assert_within(number, least, most, skip_runtime_bounds_check_because=(
                        "the plan's numbers add up to the ends of the loops"))

                for n in range(EDGE_HEAD):
                    yield n, n % GATHERS, None, None, None
                with eng.Fori(EDGE_HEAD, offset, GATHERS) as i:
                    for g in range(GATHERS):
                        yield pair(i + g, EDGE_HEAD, EDGE_LOOP_END - 1), g, None, None, None
                with eng.If(lead > 0):
                    for k in range(HEAD):
                        n = pair(offset_beyond + (LEAST + k), LEAST + k, EDGE_LOOP_END - 1)
                        yield n, k % GATHERS, k, k % SLOTS, 32 * (n - SCATTER_LAG)
                    with eng.Fori(HEAD, lead, GATHERS) as i:
                        for g in range(GATHERS):
                            n = pair(i + offset + g, LEAST + HEAD, EDGE_LOOP_END - 1)
                            yield n, g, pair(i + g, HEAD, NODE_LOOP_END - 1), g % SLOTS, 32 * (n - SCATTER_LAG)
                    for n in range(EDGE_LOOP_END, PAIRS + EDGE_LAG):
                        k = pair(lead_beyond + (LEAST + n - EDGE_LOOP_END), LEAST, NODE_LOOP_END - 1)
                        yield n, n % GATHERS, k, n % SLOTS, min(everything, 32 * (n - SCATTER_LAG))
                with eng.Else():
                    for n in range(EDGE_LOOP_END, PAIRS + EDGE_LAG):
                        yield n, n % GATHERS, None, None, None
                    for k in range(HEAD):
                        yield None, None, k, k % SLOTS, everything
                with eng.Fori(HEAD, rest_end, SLOTS) as i:
                    for s in range(SLOTS):
                        yield None, None, pair(i + rest + s, HEAD, NODE_LOOP_END - 1), s, everything
                for k in range(NODE_LOOP_END, PAIRS + NODE_LAG):
                    yield None, None, k, k % SLOTS, everything

            block = c.enter_context(nc.Block())

            @block.sync
            def _(sp):
                for n, g, k, s, edges_in in edge_and_node_steps(sp):
                    if n is not None and live(n):
                        source = dst_rows[bass.ds(n * PR, PR)].rearrange("(a e) -> a e", a=1).to_broadcast([P, PR])
                        if late(n, GATHERS):
                            sp.wait_ge(same_ok, n - 3)
                        sp.dma_start(dst_row[g][:, :], source).then_inc(row_in[g], 16)
                    if k is None:
                        continue
                    if live(k):
                        base_source, neigh_source = node_rows(base, k), node_rows(neigh, k)
                        if late(k, SLOTS):
                            sp.wait_ge(x1_ok, k - 1)
                        sp.dma_start(node_tile(bt[s], k), base_source).then_inc(base_in[s], 16)
                        if late(k, SLOTS):
                            sp.wait_ge(h_ok, k - 1)
                        sp.wait_ge(scattered, edges_in)
                        sp.dma_start(node_tile(nt[s], k), neigh_source).then_inc(neigh_in[s], 16)
                    m, q = k - 1, (s + 1) % SLOTS
                    if live(m):
                        target = node_rows(x1_rows, m)
                        sp.wait_ge(x1_ok, m + 1)
                        sp.dma_start(target, node_tile(x1[q], m)).then_inc(x1_stored[q], 16)
                    m, q = k - 5, (s + 1) % SLOTS
                    if live(m):
                        target = node_rows(h2_rows, m)
                        sp.wait_ge(h2_ok, m + 1)
                        sp.dma_start(target, node_tile(h2[q], m)).then_inc(h2_stored[q], 16)
                for s in range(SLOTS):
                    sp.wait_ge(x1_stored[s], 16 * PAIRS // SLOTS)
                    sp.wait_ge(h2_stored[s], 16 * PAIRS // SLOTS)

            @block.gpsimd
            def _(pool):
                pool.memset(h2_sum[:, :, :], 0.0).then_inc(cleared, 1)
                pool.memset(h2_squares[:, :, :], 0.0).then_inc(cleared, 1)
                pool.wait_ge(cleared, 2)
                for n, g, k, s, _ in edge_and_node_steps(pool):
                    if n is not None:
                        if live(n):
                            pool.wait_ge(gather_i_ok, n + 1)
                            if late(n, GATHERS):
                                pool.wait_ge(normed_ok, n - 3)
                            settle(pool)
                            for j in range(2):
                                pool.indirect_dma_start(
                                    out=xe[g][:, j, :], out_offset=None, in_=base,
                                    in_offset=bass.IndirectOffsetOnAxis(ap=gather_i[g][:, j:j + 1], axis=0),
                                ).then_inc(x_in[g], 16)
                        m, q = n - 6, (g + 2) % GATHERS
                        if live(m):
                            pool.wait_ge(rows_ok, m + 1)
                            pool.wait_ge(index_ok, m + 1)
                            if late(m, 1):
                                pool.wait_ge(scattered, 32 * m)
                            settle(pool)
                            for j in range(2):
                                pool.indirect_dma_start(
                                    out=neigh, out_offset=bass.IndirectOffsetOnAxis(ap=scatter_slot[q][:, j:j + 1], axis=0),
                                    in_=rows[q][:, j, :], in_offset=None, compute_op=ALU.add).then_inc(scattered, 16)
                    if k is not None and live(k - 5):
                        m, q = k - 5, (s + 1) % SLOTS
                        part = (lambda t: t[0:TAIL, 0, :]) if last(m) else (lambda t: t[:, :, :])
                        pool.wait_ge(h2_ok, m + 1)
                        pool.wait_ge(square_ok, m + 1)
                        if late(m, 1):
                            pool.wait_ge(sums_ok, m)
                        pool.tensor_tensor(part(h2_sum), part(h2_sum), part(h2[q]), ALU.add)
                        pool.tensor_tensor(part(h2_squares), part(h2_squares), part(square[q]), ALU.add).then_inc(sums_ok, 1)

            @block.tensor
            def _(pe):
                for n, g, k, s, _ in edge_and_node_steps(pe):
                    if k is not None and live(k - 1):
                        m, q = k - 1, (s + 1) % SLOTS
                        pe.wait_ge(h_ok, m + 1)
                        if late(m, 1):
                            pe.wait_ge(lo_ok, m)
                        for f in range(KC):
                            for r in range(2):
                                t = pe.transpose(turned[:, f, r * P:(r + 1) * P],
                                                 h[q][:, r, f * P:(f + 1) * P], ident[:, :])
                        t.then_inc(turned_ok, 1)
                    if n is not None and live(n - 4):
                        m, q = n - 4, g % SLOTS
                        pe.wait_ge(normed_lo_ok, m + 1)
                        pe.wait_ge(same_ok, m + 1)
                        if late(m, 1):
                            pe.wait_ge(rows_ok, m)
                        for i in range(2):
                            for j in range(2):
                                pe.matmul(summed[:, i, :], same[q][:, j, i * P:(i + 1) * P], normed_hi[q][:, j, :],
                                          start=(j == 0), stop=False)
                                mm = pe.matmul(summed[:, i, :], same[q][:, j, i * P:(i + 1) * P], normed_lo[q][:, j, :],
                                               start=False, stop=(j == 1))
                        mm.then_inc(summed_ok, 1)
                    if k is not None and live(k - 2):
                        m, q = k - 2, s
                        pe.wait_ge(lo_ok, m + 1)
                        if late(m, SLOTS):
                            pe.wait_ge(act_ok, m - 1)
                        for f in range(HC):
                            mm = product(pe, hidden[q][:, f, :],
                                         [(w1s[0][:, i, f * P:(f + 1) * P], w1s[1][:, i, f * P:(f + 1) * P],
                                           hi[q][:, i, :], lo[q][:, i, :]) for i in range(KC)])
                        mm.then_inc(hidden_ok, 1)
                    if k is not None and live(k - 3):
                        m, q = k - 3, (s + 1) % SLOTS
                        pe.wait_ge(act_lo_ok, m + 1)
                        if late(m, SLOTS):
                            pe.wait_ge(square_ok, m - 1)
                        for r in range(2):
                            mm = product(pe, prod[q][:, r, :],
                                         [(act_hi[q][:, f, r * P:(r + 1) * P], act_lo[q][:, f, r * P:(r + 1) * P],
                                           w2s[0][:, f, :], w2s[1][:, f, :]) for f in range(HC)])
                        mm.then_inc(prod_ok, 1)

            @block.scalar
            def _(act):
                for n, g, k, s, _ in edge_and_node_steps(act):
                    if n is not None and live(n - 4):
                        m, q = n - 4, g % SLOTS
                        act.wait_ge(normed_ok, m + 1)
                        if late(m, SLOTS):
                            act.wait_ge(summed_ok, m - 1)
                        act.copy(normed_hi[q][:, :, :], normed[q][:, :, :]).then_inc(normed_hi_ok, 1)
                    if k is not None and live(k - 2):
                        m, q = k - 2, s
                        act.wait_ge(turned_ok, m + 1)
                        if late(m, SLOTS):
                            act.wait_ge(hidden_ok, m - 1)
                        act.copy(hi[q][:, :, :], turned[:, :, :]).then_inc(hi_ok, 1)
                    if n is not None and live(n - 5):
                        m, q = n - 5, (g + 3) % GATHERS
                        act.wait_ge(summed_ok, m + 1)
                        if late(m, GATHERS):
                            act.wait_ge(scattered, 32 * (m - 3))
                        act.copy(rows[q][:, :, :], summed[:, :, :]).then_inc(rows_ok, 1)
                    if k is not None and live(k - 3):
                        m, q = k - 3, (s + 1) % SLOTS
                        act.wait_ge(hidden_ok, m + 1)
                        if late(m, SLOTS):
                            act.wait_ge(act_lo_ok, m - 1)
                        for f in range(HC):
                            a = act.activation(act_out[q][:, f, :], hidden[q][:, f, :], ACT.Relu, bias=b1_col[:, f:f + 1])
                        a.then_inc(act_ok, 1)
                    if n is not None and live(n - 3):
                        norm_root(act, n - 3, (g + 1) % SLOTS, edge_ln)
                    if k is not None and live(k - 3):
                        m, q = k - 3, (s + 1) % SLOTS
                        act.wait_ge(act_ok, m + 1)
                        if late(m, SLOTS):
                            act.wait_ge(prod_ok, m - 1)
                        act.copy(act_hi[q][:, :, :], act_out[q][:, :, :]).then_inc(act_hi_ok, 1)
                    if k is not None and live(k - 4):
                        m, q = k - 4, s
                        act.wait_ge(prod_ok, m + 1)
                        if late(m, SLOTS):
                            act.wait_ge(h2_stored[q], used_before(m, q))
                            act.wait_ge(sums_ok, m - 1)
                        act.copy(h2[q][:, :, :], prod[q][:, :, :]).then_inc(h2_ok, 1)
                        act.activation(square[q][:, :, :], prod[q][:, :, :], ACT.Square).then_inc(square_ok, 1)
                    if k is not None and live(k):
                        norm_root(act, k, s, node_ln)

            @block.vector
            def _(dve):
                dve.tensor_copy(gather_i[0][:, :], gather_cols[:, 0:2]).then_inc(gather_i_ok, 1)
                for n, g, k, s, _ in edge_and_node_steps(dve):
                    edges, nodes = n is not None and live(n - 3), k is not None and live(k)
                    if n is not None:
                        m, g3, q3 = n - 3, (g + 1) % GATHERS, (g + 1) % SLOTS
                    if edges:
                        dve.wait_ge(x_in[g3], uses(m, g3, 2, GATHERS))
                        norm_stats(dve, m, q3, edge_ln, xe[g3])
                    if k is not None and live(k - 2):
                        dve.wait_ge(hi_ok, k - 1)
                        dve.tensor_tensor(lo[s][:, :, :], turned[:, :, :], hi[s][:, :, :].bitcast(F32),
                                          ALU.subtract).then_inc(lo_ok, 1)
                    if n is not None and live(n - 4):
                        q = g % SLOTS
                        dve.wait_ge(normed_hi_ok, n - 3)
                        dve.tensor_tensor(normed_lo[q][:, :, :], normed[q][:, :, :], normed_hi[q][:, :, :].bitcast(F32),
                                          ALU.subtract).then_inc(normed_lo_ok, 1)
                    if edges:
                        norm_var(dve, m, q3, edge_ln)
                    if n is not None and live(n + 1):
                        dve.tensor_copy(gather_i[g3][:, :], gather_cols[:, bass.ds(4 * n + 4, 2)]).then_inc(gather_i_ok, 1)
                    if n is not None and live(n - 5):
                        if late(n - 5, GATHERS):
                            dve.wait_ge(scattered, 32 * (n - 8))
                        dve.tensor_copy(scatter_slot[(g + 3) % GATHERS][:, :],
                                        scatter_i[:, bass.ds(2 * (n - 5), 2)]).then_inc(index_ok, 1)
                    if nodes:
                        dve.wait_ge(base_in[s], uses(k, s))
                        norm_stats(dve, k, s, node_ln, bt[s])
                    if edges:
                        norm_rstd(dve, m, q3, edge_ln)
                        equal_edges(dve, m, dst_row[g3], same[q3], row_in[g3], uses(m, g3, 1, GATHERS), same_ok, summed_ok)
                        norm_apply(dve, m, q3, edge_ln, xe[g3], normed[q3], normed_ok)
                    if nodes:
                        norm_var(dve, k, s, node_ln)
                    if k is not None and live(k - 3):
                        q = (s + 1) % SLOTS
                        dve.wait_ge(act_hi_ok, k - 2)
                        dve.tensor_tensor(act_lo[q][:, 0:2, :], act_out[q][:, 0:2, :], act_hi[q][:, 0:2, :].bitcast(F32),
                                          ALU.subtract)
                    if nodes:
                        norm_rstd(dve, k, s, node_ln)
                    if k is not None and live(k - 3):
                        dve.tensor_tensor(act_lo[q][:, 2:HC, :], act_out[q][:, 2:HC, :], act_hi[q][:, 2:HC, :].bitcast(F32),
                                          ALU.subtract).then_inc(act_lo_ok, 1)
                    if nodes:
                        if late(k, SLOTS):
                            dve.wait_ge(x1_stored[s], used_before(k, s))
                        norm_apply(dve, k, s, node_ln, bt[s], x1[s], x1_ok)
                        dve.wait_ge(x1_ok, k + 1)
                        dve.wait_ge(neigh_in[s], uses(k, s))
                        if late(k, SLOTS):
                            dve.wait_ge(turned_ok, k - 1)
                        dve.scalar_tensor_tensor(h[s][:, :, :], x1[s][:, :, :], eps1_col[:, 0:1], nt[s][:, :, :],
                                                 ALU.mult, ALU.add).then_inc(h_ok, 1)

        bn_scale = sb("bn_scale", [P, D])
        bn_shift = sb("bn_shift", [P, D])
        with ExitStack() as c:
            gamma_b, beta_b, b2_b = (sb(name, [P, D], c=c) for name in ("gamma_b", "beta_b", "b2_b"))
            mean, second, mean_sq, bn_var, bn_root, bn_rstd, mean_b2, apart, bn_scaled = (
                sb("bn_" + name, [P, D], c=c) for name in
                "mean second mean_sq var root rstd mean_b2 apart scaled".split())
            bn_totals = ps("bn_totals", [P, 2, D], c)
            bn_loaded, bn_totals_ok, bn_var_ok, bn_root_ok, bn_chain, bn_shift_ok = sems(
                c, "bn_loaded", "bn_totals_ok", "bn_var_ok", "bn_root_ok", "bn_chain", "bn_shift_ok")
            x1 = [sb(f"e_x1{s}", [P, 2, D], c=c) for s in range(GATHERS)]
            h2 = [sb(f"e_h2{s}", [P, 2, D], c=c) for s in range(GATHERS)]
            shifted = [sb(f"e_shifted{s}", [P, 2, D], c=c) for s in range(GATHERS)]
            scaled = [sb(f"e_scaled{s}", [P, 2, D], c=c) for s in range(GATHERS)]
            y = [sb(f"e_y{s}", [P, 2, D], c=c) for s in range(GATHERS)]
            res = [sb(f"e_res{s}", [P, 2, D], c=c) for s in range(GATHERS)]
            stats = [sb(f"e_stats{s}", [P, 2, 6], c=c) for s in range(GATHERS)]
            mean_var = [sb(f"e_mean_var{s}", [P, 2, 2], c=c) for s in range(GATHERS)]
            root = [sb(f"e_root{s}", [P, 2], c=c) for s in range(GATHERS)]
            rstd = [sb(f"e_rstd{s}", [P, 2], c=c) for s in range(GATHERS)]
            off = [sb(f"e_off{s}", [P, 2], c=c) for s in range(GATHERS)]
            x1_in = sems(c, *(f"e_x1_in{s}" for s in range(GATHERS)))
            h2_in = sems(c, *(f"e_h2_in{s}" for s in range(GATHERS)))
            stored = sems(c, *(f"e_stored{s}" for s in range(GATHERS)))
            shifted_ok, scaled0_ok, scaled1_ok, y_ok, stats_ok, var_ok, root_ok, rstd_ok, off_ok, res_ok = sems(
                c, *("e_" + name for name in
                     "shifted_ok scaled0_ok scaled1_ok y_ok stats_ok var_ok root_ok rstd_ok off_ok res_ok".split()))
            block = c.enter_context(nc.Block())

            @block.sync
            def _(sp):
                for tile, row in ((gamma_b, gamma), (beta_b, beta), (b2_b, b2)):
                    sp.dma_start(tile[:, :], row.rearrange("(a d) -> a d", a=1).to_broadcast([P, D])).then_inc(bn_loaded, 16)
                for n, s in pair_steps(sp, 5, GATHERS):
                    if live(n):
                        x1_source, h2_source = node_rows(x1_rows, n), node_rows(h2_rows, n)
                        if late(n, GATHERS):
                            sp.wait_ge(shifted_ok, n - 3)
                        sp.dma_start(node_tile(x1[s], n), x1_source).then_inc(x1_in[s], 16)
                        if late(n, GATHERS):
                            sp.wait_ge(y_ok, n - 3)
                        sp.dma_start(node_tile(h2[s], n), h2_source).then_inc(h2_in[s], 16)
                    m, q = n - 5, (s + 3) % GATHERS
                    if live(m):
                        target = node_rows(out, m)
                        sp.wait_ge(res_ok, m + 1)
                        sp.dma_start(target, node_tile(res[q], m)).then_inc(stored[q], 16)
                for s in range(GATHERS):
                    sp.wait_ge(stored[s], 16 * PAIRS // GATHERS)

            @block.tensor
            def _(pe):
                for i, sums in enumerate((h2_sum, h2_squares)):
                    for r in range(2):
                        mm = pe.matmul(bn_totals[:, i, :], ones[:, :], sums[:, r, :], start=(r == 0), stop=(r == 1))
                mm.then_inc(bn_totals_ok, 1)

            @block.gpsimd
            def _(pool):
                pool.wait_ge(bn_shift_ok, 1)
                for n, s in pair_steps(pool, 0, GATHERS):
                    if late(n, GATHERS):
                        pool.wait_ge(y_ok, n - 3)
                    pool.wait_ge(x1_in[s], uses(n, s, 1, GATHERS))
                    pool.tensor_tensor(shifted[s][:, :, :], x1[s][:, :, :], twice(bn_shift), ALU.add).then_inc(shifted_ok, 1)
                    pool.wait_ge(h2_in[s], uses(n, s, 1, GATHERS))
                    pool.tensor_tensor(scaled[s][:, 1, :], h2[s][:, 1, :], bn_scale[:, :], ALU.mult).then_inc(scaled1_ok, 1)

            @block.scalar
            def _(act):
                act.wait_ge(bn_var_ok, 1)
                act.activation(bn_root[:, :], bn_var[:, :], ACT.Sqrt).then_inc(bn_root_ok, 1)
                for n, s in pair_steps(act, 1, GATHERS):
                    if live(n):
                        act.wait_ge(var_ok, n + 1)
                        if late(n, GATHERS):
                            act.wait_ge(rstd_ok, n - 3)
                        act.activation(root[s][:, :], mean_var[s][:, :, 1], ACT.Sqrt, bias=eps_col[:, 0:1]).then_inc(root_ok, 1)
                    m, q = n - 1, (s + 3) % GATHERS
                    if live(m):
                        act.wait_ge(off_ok, m + 1)
                        if late(m, GATHERS):
                            act.wait_ge(stored[q], used_before(m, q, 1, GATHERS))
                        for r in range(2):
                            t = act.activation(res[q][:, r, :], y[q][:, r, :], ACT.Identity, bias=off[q][:, r:r + 1],
                                               scale=rstd[q][:, r:r + 1])
                        t.then_inc(res_ok, 1)

            @block.vector
            def _(dve):
                dve.wait_ge(bn_loaded, 48)
                dve.wait_ge(bn_totals_ok, 1)
                dve.tensor_scalar(mean[:, :], bn_totals[:, 0, :], 1.0 / N, None, ALU.mult).then_inc(bn_chain, 1)
                dve.tensor_scalar(second[:, :], bn_totals[:, 1, :], 1.0 / N, EPS, ALU.mult, ALU.add).then_inc(bn_chain, 1)
                dve.wait_ge(bn_chain, 2)
                dve.tensor_tensor(mean_sq[:, :], mean[:, :], mean[:, :], ALU.mult).then_inc(bn_chain, 1)
                dve.tensor_tensor(mean_b2[:, :], mean[:, :], b2_b[:, :], ALU.add).then_inc(bn_chain, 1)
                dve.wait_ge(bn_chain, 4)
                dve.tensor_tensor(bn_var[:, :], second[:, :], mean_sq[:, :], ALU.subtract).then_inc(bn_var_ok, 1)
                dve.tensor_tensor(apart[:, :], b2_b[:, :], mean_b2[:, :], ALU.subtract).then_inc(bn_chain, 1)
                dve.wait_ge(bn_root_ok, 1)
                dve.reciprocal(bn_rstd[:, :], bn_root[:, :]).then_inc(bn_chain, 1)
                dve.wait_ge(bn_chain, 6)
                dve.tensor_tensor(bn_scale[:, :], bn_rstd[:, :], gamma_b[:, :], ALU.mult).then_inc(bn_chain, 1)
                dve.wait_ge(bn_chain, 7)
                dve.tensor_tensor(bn_scaled[:, :], apart[:, :], bn_scale[:, :], ALU.mult).then_inc(bn_chain, 1)
                dve.wait_ge(bn_chain, 8)
                dve.tensor_tensor(bn_shift[:, :], bn_scaled[:, :], beta_b[:, :], ALU.add).then_inc(bn_shift_ok, 1)
                for n, s in pair_steps(dve, 2, GATHERS):
                    m, q = n - 1, (s + 3) % GATHERS
                    k, t = n - 2, (s + 2) % GATHERS
                    if live(n):
                        dve.wait_ge(h2_in[s], uses(n, s, 1, GATHERS))
                        dve.tensor_tensor(scaled[s][:, 0, :], h2[s][:, 0, :], bn_scale[:, :], ALU.mult).then_inc(scaled0_ok, 1)
                    if live(m):
                        dve.wait_ge(y_ok, m + 1)
                        for r in range(2):
                            last_stats = dve.bn_stats(stats[q][:, r, :], y[q][:, r, :])
                        last_stats.then_inc(stats_ok, 1)
                    if live(k):
                        dve.wait_ge(root_ok, k + 1)
                        if late(k, GATHERS):
                            dve.wait_ge(res_ok, k - 3)
                        dve.reciprocal(rstd[t][:, :], root[t][:, :]).then_inc(rstd_ok, 1)
                    if live(n):
                        dve.wait_ge(scaled0_ok, n + 1)
                        dve.wait_ge(scaled1_ok, n + 1)
                        dve.wait_ge(shifted_ok, n + 1)
                        if late(n, GATHERS):
                            dve.wait_ge(res_ok, n - 3)
                        dve.tensor_tensor(y[s][:, :, :], scaled[s][:, :, :], shifted[s][:, :, :], ALU.add).then_inc(y_ok, 1)
                    if live(k):
                        dve.wait_ge(rstd_ok, k + 1)
                        dve.scalar_tensor_tensor(off[t][:, :], mean_var[t][:, :, 0], -1.0, rstd[t][:, :],
                                                 ALU.mult, ALU.mult).then_inc(off_ok, 1)
                    if live(m):
                        dve.wait_ge(stats_ok, m + 1)
                        settle(dve)
                        for r in range(2):
                            last_var = dve.bn_aggr(mean_var[q][:, r, :], stats[q][:, r, :])
                        last_var.then_inc(var_ok, 1)


def kernel(**inputs):
    import concourse.bacc as bacc
    import numpy as np
    from concourse.bass_utils import run_bass_kernel_spmd

    nc = bacc.Bacc("TRN2", target_bir_lowering=False, num_devices=1)
    x = np.ascontiguousarray(inputs["x"])
    src, dst = np.asarray(inputs["src"]), np.asarray(inputs["dst"])
    nodes, edges = x.shape[0], src.shape[0]
    assert edges == nodes
    pairs = -(-edges // PR)
    pad = pairs * PR - edges

    def columns(a, fill):
        whole = np.concatenate([a, np.full(pad, fill, a.dtype)])
        return np.ascontiguousarray(whole.reshape(-1, P).T)

    gathers = np.stack([columns(src, 0).reshape(P, pairs, 2), columns(dst, 0).reshape(P, pairs, 2)], axis=2)
    arrays = {"x": x, "gather_cols": np.ascontiguousarray(gathers.reshape(P, -1)),
              "dst_cols": columns(dst, nodes), "dst_rows": np.concatenate([dst, np.full(pad, nodes, dst.dtype)])}
    for name in ("W_key", "W_query", "W_value", "W_skip", "bias"):
        arrays["L0_" + name] = np.ascontiguousarray(inputs["L0_gnn_" + name])
    for name in ("eps", "W1", "b1", "W2", "b2", "gamma", "beta"):
        arrays["L1_" + name] = np.ascontiguousarray(inputs["L1_gnn_" + name])
    arrays = {f"in_{name}": a for name, a in arrays.items()}
    args = [nc.dram_tensor(name, a.shape, mybir.dt.from_np(a.dtype), kind="ExternalInput").ap()
            for name, a in arrays.items()]
    args.append(nc.dram_tensor("out_rows", x.shape, F32, kind="ExternalOutput").ap())
    gnn_kernel(nc, *args)
    return run_bass_kernel_spmd(nc, [arrays], core_ids=[0]).results[0]["out_rows"]
```
